# Optimizing a Trainium2 kernel written in Bass

```python
import numpy as np
import jax
import jax.numpy as jnp

def _softmax(x, axis=-1):
    return jax.nn.softmax(x, axis=axis)

def _gelu(x):
    return jax.nn.gelu(x, approximate=True)

def _silu(x):
    return jax.nn.silu(x)

def _sigmoid(x):
    return jax.nn.sigmoid(x)

def _layernorm(x, axis=-1, eps=1e-05):
    m = jnp.mean(x, axis=axis, keepdims=True)
    v = jnp.var(x, axis=axis, keepdims=True)
    return (x - m) / jnp.sqrt(v + eps)

def _scatter_add(tgt, idx, src, axis=0):
    return tgt.at[idx].add(src)

def _segment_sum(src, seg, n):
    return jax.ops.segment_sum(src, seg, n)
kernel_name = 'mk_adj_preln_d4_adj_r2_6950bc'

def setup_inputs(seed: int=0):
    np.random.seed(seed)
    _w = jnp.asarray

    def _rec_inputs():
        import jax
        import jax.numpy as jnp
        _gk = jax.random.key(seed)
        x = -0.000929 + 1 * jax.random.normal(jax.random.fold_in(_gk, 1), (3327, 64), jnp.float32)
        _a = jax.random.bernoulli(jax.random.fold_in(_gk, 2), 0.00480914, (3327, 3327))
        _a = jnp.logical_or(_a, jnp.swapaxes(_a, -1, -2))
        _a = jnp.logical_or(_a, jnp.eye(3327, dtype=bool))
        _af = _a.astype(jnp.float32)
        adj = _af
        return (x, adj)
    x, adj = _rec_inputs()

    def _L0_gnn_setup():
        import jax, jax.numpy as jnp
        import numpy as np
        N, D_IN, D_OUT = (8192, 64, 64)
        AVG_DEG = 32.0
        L2_EPS = 1e-12
        key = jax.random.key(seed)
        kx, ka, kw, kb = jax.random.split(key, 4)
        X = jax.random.normal(kx, (N, D_IN), dtype=jnp.float32)
        adj = (jax.random.uniform(ka, (N, N)) < AVG_DEG / N).astype(jnp.float32)
        bound = 1.0 / np.sqrt(2 * D_IN)
        W = jax.random.uniform(kw, (2 * D_IN, D_OUT), dtype=jnp.float32, minval=-bound, maxval=bound)
        b = jax.random.uniform(kb, (D_OUT,), dtype=jnp.float32, minval=-bound, maxval=bound)
        return {'X': X, 'adj': adj, 'W': W, 'b': b}
    _L0_gnn_all = _L0_gnn_setup()
    _L0_gnn_in = {k: v for k, v in _L0_gnn_all.items() if k in ('W', 'b')}
    del _L0_gnn_all

    def _L1_gnn_setup():
        import jax, jax.numpy as jnp
        import numpy as np
        N, D, H = (8192, 64, 128)
        GAIN = 0.2
        key = jax.random.key(seed)
        ks = jax.random.split(key, 6)
        X = jax.random.normal(ks[0], (N, D), dtype=jnp.float32)
        t = jax.random.uniform(ks[1], (1,), dtype=jnp.float32)
        Wt = jax.random.uniform(ks[2], (N, N), dtype=jnp.float32)
        B = GAIN * jnp.eye(D, dtype=jnp.float32) + 0.01 * jax.random.normal(ks[3], (D, D), dtype=jnp.float32)
        W1 = jax.random.normal(ks[4], (D + 1, H), dtype=jnp.float32) * (1.0 / np.sqrt(D + 1))
        b1 = jnp.zeros((H,), dtype=jnp.float32)
        W2 = jax.random.normal(ks[5], (H, D), dtype=jnp.float32) * (1.0 / np.sqrt(H))
        b2 = jnp.zeros((D,), dtype=jnp.float32)
        return {'X': X, 't': t, 'Wt': Wt, 'B': B, 'W1': W1, 'b1': b1, 'W2': W2, 'b2': b2}
    _L1_gnn_all = _L1_gnn_setup()
    _L1_gnn_in = {k: v for k, v in _L1_gnn_all.items() if k in ('t', 'B', 'W1', 'b1', 'W2', 'b2')}
    del _L1_gnn_all

    def _L2_gnn_setup():
        import jax, jax.numpy as jnp
        import numpy as np
        CURV = 1.0
        MIN_NORM = 1e-15
        TANH_CLIP = 1.0 - 1e-05

        def _mobius_add(x, y, c):
            x2 = jnp.sum(x * x, axis=-1, keepdims=True)
            y2 = jnp.sum(y * y, axis=-1, keepdims=True)
            xy = jnp.sum(x * y, axis=-1, keepdims=True)
            num = (1.0 + 2.0 * c * xy + c * y2) * x + (1.0 - c * x2) * y
            den = 1.0 + 2.0 * c * xy + c ** 2 * x2 * y2
            return num / jnp.maximum(den, MIN_NORM)

        def _logmap(x, y, c):
            sub = _mobius_add(-x, y, c)
            sub_norm = jnp.maximum(jnp.linalg.norm(sub, axis=-1, keepdims=True), MIN_NORM)
            x2 = jnp.sum(x * x, axis=-1, keepdims=True)
            lam_x = 2.0 / jnp.maximum(1.0 - c * x2, MIN_NORM)
            sqrt_c = jnp.sqrt(c)
            arg = jnp.clip(sqrt_c * sub_norm, 0.0, TANH_CLIP)
            return 2.0 / (sqrt_c * lam_x) * jnp.arctanh(arg) * sub / sub_norm

        def _expmap(x, v, c):
            v_norm = jnp.maximum(jnp.linalg.norm(v, axis=-1, keepdims=True), MIN_NORM)
            x2 = jnp.sum(x * x, axis=-1, keepdims=True)
            lam_x = 2.0 / jnp.maximum(1.0 - c * x2, MIN_NORM)
            sqrt_c = jnp.sqrt(c)
            second = jnp.tanh(sqrt_c * lam_x * v_norm / 2.0) * v / (sqrt_c * v_norm)
            return _mobius_add(x, second, c)
        key = jax.random.key(seed)
        k1, k2, k3 = jax.random.split(key, 3)
        N, C_IN, C_OUT = (768, 64, 64)
        x = jax.random.normal(k1, (N, C_IN), dtype=jnp.float32) * 0.03
        adj = (jax.random.uniform(k2, (N, N)) < 0.02).astype(jnp.float32)
        bound = 1.0 / np.sqrt(C_IN)
        weight = jax.random.uniform(k3, (C_IN, C_OUT), dtype=jnp.float32, minval=-bound, maxval=bound)
        bias = jnp.zeros((C_OUT,), dtype=jnp.float32)
        return {'x': x, 'adj': adj, 'weight': weight, 'bias': bias}
    _L2_gnn_all = _L2_gnn_setup()
    _L2_gnn_in = {k: v for k, v in _L2_gnn_all.items() if k in ('weight', 'bias')}
    del _L2_gnn_all

    def _L3_gnn_setup():
        import jax, jax.numpy as jnp
        import numpy as np
        N, D_IN, D_OUT = (4096, 64, 64)
        MAX_NEIGH = 100
        DECAY = 0.5
        key = jax.random.key(seed)
        k1, k2, k3, k4 = jax.random.split(key, 4)
        stdv = 1.0 / np.sqrt(D_OUT)
        inputs = {'input': jax.random.normal(k1, (N, D_IN), dtype=jnp.float32), 'adj': jax.random.randint(k2, (N, N), 0, 2).astype(jnp.float32), 'weight': jax.random.uniform(k3, (D_IN, D_OUT), minval=-stdv, maxval=stdv, dtype=jnp.float32), 'bias': jax.random.uniform(k4, (D_OUT,), minval=-stdv, maxval=stdv, dtype=jnp.float32)}
        return inputs
    _L3_gnn_all = _L3_gnn_setup()
    _L3_gnn_in = {k: v for k, v in _L3_gnn_all.items() if k in ('weight', 'bias')}
    del _L3_gnn_all
    return {'x': x, 'adj': adj, 'L0_gnn_W': _L0_gnn_in['W'], 'L0_gnn_b': _L0_gnn_in['b'], 'L1_gnn_t': _L1_gnn_in['t'], 'L1_gnn_B': _L1_gnn_in['B'], 'L1_gnn_W1': _L1_gnn_in['W1'], 'L1_gnn_b1': _L1_gnn_in['b1'], 'L1_gnn_W2': _L1_gnn_in['W2'], 'L1_gnn_b2': _L1_gnn_in['b2'], 'L2_gnn_weight': _L2_gnn_in['weight'], 'L2_gnn_bias': _L2_gnn_in['bias'], 'L3_gnn_weight': _L3_gnn_in['weight'], 'L3_gnn_bias': _L3_gnn_in['bias']}

def reference(x, adj, L0_gnn_W, L0_gnn_b, L1_gnn_t, L1_gnn_B, L1_gnn_W1, L1_gnn_b1, L1_gnn_W2, L1_gnn_b2, L2_gnn_weight, L2_gnn_bias, L3_gnn_weight, L3_gnn_bias):
    import jax
    import jax.numpy as jnp

    def _L0_gnn_ref(X, adj, W, b):
        import jax, jax.numpy as jnp
        import numpy as np
        N, D_IN, D_OUT = (8192, 64, 64)
        AVG_DEG = 32.0
        L2_EPS = 1e-12
        deg = jnp.clip(jnp.sum(adj, axis=1, keepdims=True) + 1.0, 1.0, None)
        h_neigh = (adj @ X + X) / deg
        concat = jnp.concatenate([X, h_neigh], axis=1)
        z = concat @ W + b
        out = jax.nn.relu(z)
        norm = jnp.linalg.norm(out, axis=1, keepdims=True)
        return out / jnp.maximum(norm, L2_EPS)

    def _L1_gnn_ref(X, t, Wt, B, W1, b1, W2, b2):
        import jax, jax.numpy as jnp
        import numpy as np
        N, D, H = (8192, 64, 128)
        GAIN = 0.2
        n = X.shape[0]
        tcol = jnp.broadcast_to(t.reshape(1, 1), (n, 1))
        h = jnp.tanh(jnp.concatenate([X, tcol], axis=1) @ W1 + b1)
        u_intra = h @ W2 + b2
        XB = X @ B.T
        u_comm = Wt @ XB - jnp.sum(Wt, axis=1, keepdims=True) * XB
        return u_intra + u_comm

    def _L2_gnn_ref(x, adj, weight, bias):
        import jax, jax.numpy as jnp
        import numpy as np
        CURV = 1.0
        MIN_NORM = 1e-15
        TANH_CLIP = 1.0 - 1e-05

        def _mobius_add(x, y, c):
            x2 = jnp.sum(x * x, axis=-1, keepdims=True)
            y2 = jnp.sum(y * y, axis=-1, keepdims=True)
            xy = jnp.sum(x * y, axis=-1, keepdims=True)
            num = (1.0 + 2.0 * c * xy + c * y2) * x + (1.0 - c * x2) * y
            den = 1.0 + 2.0 * c * xy + c ** 2 * x2 * y2
            return num / jnp.maximum(den, MIN_NORM)

        def _logmap(x, y, c):
            sub = _mobius_add(-x, y, c)
            sub_norm = jnp.maximum(jnp.linalg.norm(sub, axis=-1, keepdims=True), MIN_NORM)
            x2 = jnp.sum(x * x, axis=-1, keepdims=True)
            lam_x = 2.0 / jnp.maximum(1.0 - c * x2, MIN_NORM)
            sqrt_c = jnp.sqrt(c)
            arg = jnp.clip(sqrt_c * sub_norm, 0.0, TANH_CLIP)
            return 2.0 / (sqrt_c * lam_x) * jnp.arctanh(arg) * sub / sub_norm

        def _expmap(x, v, c):
            v_norm = jnp.maximum(jnp.linalg.norm(v, axis=-1, keepdims=True), MIN_NORM)
            x2 = jnp.sum(x * x, axis=-1, keepdims=True)
            lam_x = 2.0 / jnp.maximum(1.0 - c * x2, MIN_NORM)
            sqrt_c = jnp.sqrt(c)
            second = jnp.tanh(sqrt_c * lam_x * v_norm / 2.0) * v / (sqrt_c * v_norm)
            return _mobius_add(x, second, c)
        c = CURV
        deg = jnp.maximum(adj.sum(axis=1, keepdims=True), 1e-08)
        w = adj / deg
        log_ij = _logmap(x[:, None, :], x[None, :, :], c)
        agg = jnp.einsum('ij,ijc->ic', w, log_ij)
        transformed = agg @ weight + bias
        origin = jnp.zeros_like(transformed)
        return _expmap(origin, transformed, c)

    def _L3_gnn_ref(input, adj, weight, bias):
        import jax, jax.numpy as jnp
        import numpy as np
        N, D_IN, D_OUT = (4096, 64, 64)
        MAX_NEIGH = 100
        DECAY = 0.5
        support = input @ weight
        mask = (adj != 0).astype(support.dtype)
        rank = jnp.cumsum(mask, axis=1)
        deg = rank[:, -1:]
        k = jnp.minimum(deg, float(MAX_NEIGH))
        pos = rank - (deg - k)
        w = mask * jnp.where(pos > 0, DECAY ** (k - pos), 0.0)
        out = w @ support + bias
        return out
    h = jnp.maximum(_layernorm(x, axis=-1), 0.0)
    x = x + _L0_gnn_ref(h, adj, L0_gnn_W, L0_gnn_b)
    h = jnp.maximum(_layernorm(x, axis=-1), 0.0)
    x = x + _L1_gnn_ref(h, L1_gnn_t, adj, L1_gnn_B, L1_gnn_W1, L1_gnn_b1, L1_gnn_W2, L1_gnn_b2)
    h = jnp.maximum(_layernorm(x, axis=-1), 0.0)
    x = x + _L2_gnn_ref(h, adj, L2_gnn_weight, L2_gnn_bias)
    h = jnp.maximum(_layernorm(x, axis=-1), 0.0)
    x = x + _L3_gnn_ref(h, adj, L3_gnn_weight, L3_gnn_bias)
    return x

_drawn_inputs = setup_inputs


def setup_inputs(seed=0):
    import zlib

    import numpy as np

    out = dict(_drawn_inputs(seed))
    spreads = {'L1_gnn_b1': (0.0, 0.315), 'L1_gnn_b2': (0.0, 0.1), 'L2_gnn_bias': (0.0, 0.329)}
    factors = {}
    for name, (base, spread) in spreads.items():
        noise = np.random.default_rng([zlib.crc32(name.encode()), seed]).standard_normal(out[name].shape)
        drawn = base * np.exp(spread * noise) if base else spread * noise
        out[name] = jnp.asarray(drawn.astype(out[name].dtype))
    for name, factor in factors.items():
        out[name] = (out[name] * factor).astype(out[name].dtype)
    return out
```

```python
import concourse.bass as bass
from concourse import mybir
from contextlib import ExitStack

N = 3327
D = 64
HID = 128
P = 128
NB = 26
NP = NB * P
NC = NB // 2
CW = 2 * P
K2 = D + 2
NW = D + 1
SPL = 3 * D
EXB = 38
UB = (8, 6)
UO = (0, 8)
UT = (2, 8)
HORIZON = 100
EDGE = 16384.0
MIN_NORM = 1e-15
LN_FLOOR = 2.0 ** -63
TANH_CLIP = 1.0 - 1e-05
EPS = 1e-05
L2_EPS = 1e-12
NORM_FLOOR = 2.0 ** -22


def gnn_stack(nc, x, adj_cols, adj_mask, w_self, w_neigh, b0, t1, bt1, w11, b11, w12, b12,
              w_hyp, b_hyp, w_dec, b_dec, out):
    fp32, bf16, i16 = mybir.dt.float32, mybir.dt.bfloat16, mybir.dt.int16
    ALU, ACT = mybir.AluOpType, mybir.ActivationFunctionType
    AX = mybir.AxisListType.X
    ctx = ExitStack()
    with ctx:
        cursor = [(nc.sbuf_base + 63) // 64 * 64]

        def place(name, shape, dt=fp32):
            n = 1
            for s in shape[1:]:
                n *= s
            at = cursor[0]
            cursor[0] = at + (n * mybir.dt.size(dt) + 31) // 32 * 32
            return nc.alloc_sbuf_tensor_at(name, shape, dt, offset=at)

        def sem(name):
            return ctx.enter_context(nc.semaphore(name))

        ident = place("ident", [P, P])
        order = place("order", [P, P], bf16)
        counts = place("counts", [P, NB, NB], bf16)
        deg = place("deg", [P, NB])
        base = place("base", [P, NB, D])
        small = place("small", [P, 16, 2])
        ones_row = place("ones_row", [1, P])
        rows = place("rows", [P, 2, SPL])
        t_a = place("t_a", [P, 2, D])
        t_b = place("t_b", [P, 2, D])
        t_c = place("t_c", [P, 2, D])
        xb = place("xb", [P, 2, D])
        kept = cursor[0]
        z_spl = place("z_spl", [P, NB, SPL + NB], bf16)
        w0 = place("w0", [NW, 2 * D])
        w1b = place("w1b", [D, D])
        w1h = place("w1h", [D, HID])
        t_rows = rows[0:2, 0, 0:HID]
        t_one = place("t_one", [2, 1])
        bias11 = place("bias11", [HID, 1])
        w1o = place("w1o", [HID, D])
        b1o = place("b1o", [1, D])
        x_in = place("x_in", [P, 2, 2, D])
        hT = place("hT", [NW, CW])
        hidT = place("hidT", [HID, CW])
        xb_spl = place("xb_spl", [P, NB, SPL], bf16)
        adj = place("adj", [P, NC, NB * CW], bf16)
        cursor[0] -= 2 * NB * CW * mybir.dt.size(bf16)
        x_all = place("x_all", [P, NB, D])
        h_pair = place("h_pair", [P, 2, 2, D])
        sq_all = place("sq_all", [P, NB, D])
        st_all = place("st_all", [P, 4, NB])
        cursor[0] = kept
        h2 = place("h2", [P, NB, D])
        pick_b = place("pick_b", [K2, P])
        w2h = place("w2h", [D, D])
        b2h = place("b2h", [1, D])
        w3d = place("w3d", [D, D])
        b3_all = place("b3_all", [P, D])
        zero_row = place("zero_row", [1, 512])
        ident16 = place("ident16", [P, P], bf16)
        aug_l = place("aug_l", [P, 2, 2, K2])
        aug_r = place("aug_r", [P, 2, 2, K2])
        row_pair = place("row_pair", [P, 2, 2, D])
        lhs_one = place("lhs_one", [K2, 2, P])
        featT = place("featT", [D, 2, CW])
        x2 = place("x2", [P, NB])
        x_b = place("x_b", [P, NB])
        pn = place("pn", [P, 8, NB])
        late = cursor[0]
        assert late <= nc.sbuf_base + 63 + 40000
        xrow = place("xrow", [P, EXB, NW])
        lhs_aug = place("lhs_aug", [K2, NP])
        rhs_aug = place("rhs_aug", [K2, EXB * P])
        x_b_row = place("x_b_row", [P, EXB * P])
        UW = [n * P for n in UB]
        mask = [[place(f"mask{u}{k}", [P, UW[u] + 6 * P]) for k in range(2)] for u in range(2)]
        den = place("den", [P, UW[0]])
        dist = [place(f"dist{u}", [P, UW[u]]) for u in range(2)]
        inv = [place(f"inv{u}", [P, UW[u]]) for u in range(2)]
        nrm = [place(f"nrm{u}", [P, UW[u]]) for u in range(2)]
        gain = [place(f"gain{u}", [P, UW[u]]) for u in range(2)]
        p_dir = [place(f"p_dir{u}", [P, UW[u]]) for u in range(2)]
        p_tr = [place(f"p_tr{u}", [P, 6 * P]) for u in range(2)]
        behind3 = cursor[0]
        s_spl = place("s_spl", [P, NB, SPL], bf16)
        countsT = place("countsT", [NB, NP], bf16)
        later = place("later", [NB, NB, P], bf16)
        adj4 = [place("adj4_0", [P, NB * CW], bf16)]
        assert cursor[0] <= nc.sbuf_usable_end, cursor
        cursor[0] = late
        adj4.append(place("adj4_1", [P, NB * CW], bf16))
        w_exp = [place(f"w_exp{k}", [P, NB, CW], i16) for k in range(2)]
        o_buf = place("o_buf", [P, 2, 2, D])
        post = [place(f"post{k}", [P, NB, D]) for k in range(4)]
        assert cursor[0] <= behind3

        lo = ctx.enter_context(nc.psum_tensor("lo", [P, 2048], fp32))
        hi = ctx.enter_context(nc.psum_tensor("hi", [P, 2048], fp32))
        agg = lo[:, :].rearrange("p (b n) -> p b n", b=4)
        tp = hi[:, 0:512]
        mm = hi[:, 512:1024]
        ux = hi[:, 1024:1536].rearrange("p (b n) -> p b n", b=2)
        one = hi[:, 1536:2048]
        ux_bank = hi[:, 1024:1536]
        aug_ps = (tp, ux_bank)
        row_ps = (mm, one)
        dist_ps = hi[:, 0:1024]
        turn_ps = hi[:, 1024:2048].rearrange("p (k n) -> p k n", k=2)
        exp_ps = [hi[:, 0:1024], hi[:, 1024:2048]]


        def acc_at(j):
            return j * 72 + j // 7 * 8

        x_in_sem = [sem(f"x_loaded{k}") for k in range(2)]
        x_all_loaded = sem("x_all_loaded")
        weights_loaded = sem("weights_loaded")
        adj_loaded = [sem(f"adj_loaded{k}") for k in range(2)]
        consts_made = sem("consts_made")
        dve_step = sem("dve_step")
        act_step = sem("act_step")
        pool_step = sem("pool_step")
        var_ready = sem("var_ready")
        root_ready = sem("root_ready")
        h_ready = sem("h_ready")
        turned = sem("turned")
        hT_ready = sem("hT_ready")
        z_ready = sem("z_ready")
        z_split = sem("z_split")
        agg_ready = sem("agg_ready")
        agg_read = sem("agg_read")
        hid_ready = sem("hid_ready")
        tanh_ready = sem("tanh_ready")
        ux_ready = sem("ux_ready")
        base_ready = sem("base_ready")
        bias_ps_ready = sem("bias_ps_ready")
        bias_ready = sem("bias_ready")
        rows_made = sem("rows_made")
        h2_ready = sem("h2_ready")
        x2_ready = sem("x2_ready")
        STEPS1, STEPS2 = 26, 7
        mask_loaded = [[sem(f"mask_loaded{u}{k}") for k in range(2)] for u in range(2)]
        late_loaded = sem("late_loaded")
        late_made = sem("late_made")
        aug_made = sem("aug_made")
        aug_turned = sem("aug_turned")
        aug_copied = sem("aug_copied")
        row_ready = sem("row_ready")
        row_copied = sem("row_copied")
        wrapped = sem("wrapped")
        lhs_copied = sem("lhs_copied")
        dist_ready = sem("dist_ready")
        apart = sem("apart")
        prod_ready = sem("prod_ready")
        inv_ready = sem("inv_ready")
        nrm_ready = sem("nrm_ready")
        logs_ready = sem("logs_ready")
        atanh_ready = sem("atanh_ready")
        gain_ready = sem("gain_ready")
        dir_ready = sem("dir_ready")
        turn_ready = sem("turn_ready")
        tr_ready = sem("tr_ready")
        dir_used = sem("dir_used")
        tr_used = sem("tr_used")
        pair_ready = sem("pair_ready")
        pair_turned = sem("pair_turned")
        feat_ready = sem("feat_ready")
        lin_ready = sem("lin_ready")
        lin_read = sem("lin_read")
        x3_ready = sem("x3_ready")
        counts_turned = sem("counts_turned")
        counts_copied = sem("counts_copied")
        nv_ready = sem("nv_ready")
        tanh3_ready = sem("tanh3_ready")
        adj4_loaded = [sem(f"adj4_loaded{k}") for k in range(2)]
        exps_made = [sem(f"exps_made{k}") for k in range(2)]
        exps_read = [sem(f"exps_read{k}") for k in range(2)]
        out_made = sem("out_made")
        out_sent = [sem(f"out_sent{k}") for k in range(2)]
        block = ctx.enter_context(nc.Block())

        class Chain:

            def __init__(self, eng, s):
                self.eng, self.s, self.n, self.base = eng, s, 0, 0

            def __call__(self, ins):
                ins.then_inc(self.s, 1)
                self.n += 1
                self.eng.wait_ge(self.s, self.base + self.n)

            def turn(self, start, index, steps):
                self.base, self.n = start + index * steps, 0

        def each_pair(eng, body):
            body(0, 0)
            body(1, 1)
            with eng.Fori(2, NC - 1, 2) as c:
                body(c, 0)
                body(c + 1, 1)
            body(NC - 1, 0)

        UNITS = 4 * NC
        GROUP = [(j, min(4, NB - j)) for j in range(0, NB, 4)]
        GROUPS = ((len(GROUP) + 1) // 2, len(GROUP) // 2)
        W_SHIFT = 128.0 * HORIZON - EDGE

        def each_unit(eng, body):
            for t in range(4):
                body(t, t % 2)
            with eng.Fori(1, NC) as s:
                for t in range(4):
                    body(4 * s + t, t % 2)

        def wide(v, n=D):
            return v.unsqueeze(2).broadcast_to([P, v.shape[1], n])

        def pair(t, c):
            return t[:, bass.ds(2 * c, 2)]

        @block.sync
        def _(sp):
            sp.dma_start(x_all[:, :, :], x).then_inc(x_all_loaded, 16)
            for dst, src in ((w0, (w_self, w_neigh, b0)),):
                sp.dma_start(dst[0:D, 0:D], src[0]).then_inc(weights_loaded, 16)
                sp.dma_start(dst[0:D, D:2 * D], src[1]).then_inc(weights_loaded, 16)
                sp.dma_start(dst[D:NW, 0:D], src[2]).then_inc(weights_loaded, 16)
            sp.dma_start(w1b[:, :], bt1).then_inc(weights_loaded, 16)
            sp.dma_start(w1h[:, :], w11[0:D, :]).then_inc(weights_loaded, 16)
            sp.dma_start(t_rows[0:1], w11[D:NW, :]).then_inc(weights_loaded, 16)
            sp.dma_start(t_rows[1:2], b11).then_inc(weights_loaded, 16)
            sp.dma_start(t_one[:, :], t1).then_inc(weights_loaded, 16)
            sp.dma_start(w1o[:, :], w12).then_inc(weights_loaded, 16)
            sp.dma_start(b1o[:, :], b12).then_inc(weights_loaded, 16)

            def load_x(c, q):
                if not isinstance(c, int) or c >= 2:
                    sp.wait_ge(base_ready, c - 1)
                sp.dma_start(x_in[:, q], pair(x, c)).then_inc(x_in_sem[q], 16)

            load_x(0, 0)
            load_x(1, 1)
            with sp.Fori(2, NC - 1, 2) as c:
                load_x(c, 0)
                load_x(c + 1, 1)
            load_x(NC - 1, 0)

            sp.wait_ge(h2_ready, NC)
            sp.dma_start(w2h[:, :], w_hyp).then_inc(late_loaded, 16)
            sp.dma_start(b2h[:, :], b_hyp).then_inc(late_loaded, 16)
            sp.dma_start(w3d[:, :], w_dec).then_inc(late_loaded, 16)
            sp.dma_start(b3_all[:, :], b_dec.broadcast_to([P, D])).then_inc(late_loaded, 16)

            def load_mask(i, r, u, s):
                if not isinstance(s, int) or s >= 1:
                    sp.wait_ge(tr_ready, 2 * (4 * s + 2 * r + u) - 6)
                at = u * (UW[0] + 6 * P)
                sp.dma_start(mask[u][r][:, :], adj_mask[i, :, at:at + UW[u] + 6 * P]) \
                    .then_inc(mask_loaded[u][r], 16)

            for r in range(2):
                for u in range(2):
                    load_mask(r, r, u, 0)
            with sp.Fori(1, NC) as s:
                for r in range(2):
                    for u in range(2):
                        load_mask(2 * s + r, r, u, s)

            def send(c, q):
                sp.wait_ge(out_made, c + 1)
                sp.dma_start(pair(out, c), o_buf[:, q]).then_inc(out_sent[q], 16)

            each_pair(sp, send)
            sp.wait_ge(out_sent[0], (NC + 1) // 2 * 16)
            sp.wait_ge(out_sent[1], NC // 2 * 16)

        @block.gpsimd
        def _(pool):
            def load_adj(c, q):
                pool.dma_start(adj[:, c], adj_cols[c]).then_inc(adj_loaded[q], 16)

            load_adj(0, 0)
            load_adj(1, 1)
            step = Chain(pool, pool_step)
            step(pool.memset(ident[:, :], 0.0))
            step(pool.affine_select(out=ident[:, :], in_=ident[:, :], compare_op=ALU.not_equal, fill=1.0,
                                    base=0, pattern=[[-1, P]], channel_multiplier=1))
            pool.memset(ones_row[:, :], 1.0).then_inc(consts_made, 1)
            hot = z_spl[:, :, SPL:SPL + NB]
            step(pool.memset(hot, 0.0))
            step(pool.affine_select(out=hot, in_=hot, compare_op=ALU.not_equal, fill=1.0,
                                    base=0, pattern=[[1, NB], [-1, NB]], channel_multiplier=0))
            step(pool.memset(order[:, :], 0.0))
            step(pool.affine_select(out=order[:, :], in_=order[:, :], compare_op=ALU.is_ge, fill=-128.0,
                                    base=0, pattern=[[1, P]], channel_multiplier=-1))
            pool.affine_select(out=order[:, :], in_=order[:, :], compare_op=ALU.not_equal, fill=EDGE,
                               base=0, pattern=[[-1, P]], channel_multiplier=1).then_inc(consts_made, 1)

            def next_adj(c, q):
                pool.wait_ge(adj_loaded[q], (c // 2) * 16)
                load_adj(c, q)

            with pool.Fori(2, NC - 3, 2) as c:
                next_adj(c, 0)
                next_adj(c + 1, 1)
            next_adj(NC - 3, 0)
            pool.wait_ge(z_split, NC)
            next_adj(NC - 2, 1)
            next_adj(NC - 1, 0)


            pool.wait_ge(h2_ready, NC)
            step(pool.memset(pick_b[:, :], 0.0))
            step(pool.affine_select(out=pick_b[:, :], in_=pick_b[:, :], compare_op=ALU.not_equal, fill=1.0,
                                    base=-D, pattern=[[0, P]], channel_multiplier=1))
            pool.affine_select(out=pick_b[:, :], in_=pick_b[:, :], compare_op=ALU.not_equal, fill=-1.0,
                               base=-D - 1, pattern=[[0, P]], channel_multiplier=1).then_inc(late_made, 1)
            step(pool.memset(ident16[:, :], 0.0))
            pool.affine_select(out=ident16[:, :], in_=ident16[:, :], compare_op=ALU.not_equal, fill=1.0,
                               base=0, pattern=[[-1, P]], channel_multiplier=1).then_inc(late_made, 1)
            step(pool.memset(later[:, :, :], 0.0))
            pool.affine_select(out=later[:, :, :], in_=later[:, :, :], compare_op=ALU.is_ge, fill=-128.0,
                               base=0, pattern=[[1, NB], [0, P]], channel_multiplier=-1).then_inc(late_made, 1)

            def product(t, u):
                pool.wait_ge(apart, t + 1)
                if not isinstance(t, int) or t >= 2:
                    pool.wait_ge(gain_ready, t - 1)
                pool.tensor_tensor(inv[u][:, :], den[:, 0:UW[u]], dist[u][:, :], ALU.mult).then_inc(prod_ready, 1)

            def twice_atanh(t, u):
                pool.wait_ge(logs_ready, t + 1)
                pool.tensor_tensor(gain[u][:, :], gain[u][:, :], nrm[u][:, :], ALU.subtract) \
                    .then_inc(atanh_ready, 1)

            def unit(t, u):
                product(t, u)
                if not isinstance(t, int) or t >= 1:
                    twice_atanh(t - 1, 1 - u)

            def load_adj4(c, q):
                pool.dma_start(adj4[q][:, :], adj_cols[c]).then_inc(adj4_loaded[q], 16)

            load_adj4(0, 0)
            each_unit(pool, unit)
            twice_atanh(UNITS - 1, 1)
            pool.wait_ge(tr_used, UNITS)
            load_adj4(1, 1)

            def next_adj4(c, q):
                pool.wait_ge(exps_made[0], GROUPS[0] * (c - 1))
                pool.wait_ge(exps_made[1], GROUPS[1] * (c - 1))
                load_adj4(c, q)

            with pool.Fori(2, NC - 1, 2) as c:
                next_adj4(c, 0)
                next_adj4(c + 1, 1)
            next_adj4(NC - 1, 0)

        @block.scalar
        def _(act):
            step = Chain(act, act_step)

            def root(n, dst, src):
                act.wait_ge(var_ready, n + 1)
                act.activation(dst, src, ACT.Sqrt).then_inc(root_ready, 1)

            root(0, st_all[:, 2, :], st_all[:, 1, :])
            act.wait_ge(bias_ps_ready, 1)
            act.activation(bias11[:, :], one[:, 0:1], ACT.Copy).then_inc(bias_ready, 1)

            def copy_hT(n):
                act.wait_ge(turned, n + 1)
                act.activation(hT[0:D, :], tp[0:D, 0:CW], ACT.Copy).then_inc(hT_ready, 1)

            def products0(c, q):
                if not isinstance(c, int) or c >= 1:
                    act.wait_ge(z_ready, c)
                copy_hT(c)

            products0(0, 0)
            with act.Fori(1, NC) as c:
                products0(c, 0)

            def layer12(c, q):
                root(2 * c + 1, small[:, 4, :], small[:, 3, :])
                root(2 * c + 2, small[:, 9, :], small[:, 8, :])
                copy_hT(NC + c)
                act.wait_ge(hid_ready, c + 1)
                act.activation(hidT[:, :], mm[:, 0:CW], ACT.Tanh, bias=bias11[:, :]).then_inc(tanh_ready, 1)

            with act.Fori(0, NC) as c:
                layer12(c, 0)
            with act.Fori(0, NC) as c:
                root(2 * NC + 1 + c, small[:, 9, :], small[:, 8, :])


            def settled():
                act.wait_ge(consts_made, 2)

            def augment(c, q):
                act.wait_ge(aug_turned, c + 1)
                settled()
                act.activation(lhs_aug[:, bass.ds(c * CW, CW)], aug_ps[q][0:K2, 0:CW], ACT.Copy)
                act.activation(rhs_aug[:, bass.ds(c * CW, CW)], aug_ps[q][0:K2, CW:2 * CW], ACT.Copy) \
                    .then_inc(aug_copied, 1)
                act.wait_ge(row_ready, c + 1)
                settled()
                act.activation(x_b_row[:, bass.ds(c * CW, CW)], row_ps[q][:, 0:CW], ACT.Copy) \
                    .then_inc(row_copied, 1)

            act.wait_ge(h2_ready, NC)
            each_pair(act, augment)
            act.preload_act_table_set("natural_log_exp_and_others")

            def block_weights(s, r):
                if not isinstance(s, int) or s >= 1:
                    act.wait_ge(dist_ready, 4 * s + 2 * r - 2)
                settled()
                act.activation(lhs_one[:, r, :], lhs_aug[:, bass.ds((2 * s + r) * P, P)], ACT.Copy) \
                    .then_inc(lhs_copied, 1)

            def inverse(t, u):
                act.wait_ge(prod_ready, t + 1)
                step(act.activation(inv[u][:, :], inv[u][:, :], ACT.Ln, bias=LN_FLOOR))
                act.activation(inv[u][:, :], inv[u][:, :], ACT.Exp, scale=-0.5).then_inc(inv_ready, 1)

            def logs(t, u):
                act.wait_ge(nrm_ready, t + 1)
                act.activation(gain[u][:, :], nrm[u][:, :], ACT.Ln, bias=1.0)
                act.activation(nrm[u][:, :], nrm[u][:, :], ACT.Ln, scale=-1.0, bias=1.0).then_inc(logs_ready, 1)

            def units(s):
                for r in range(2):
                    for u in range(2):
                        t = 4 * s + 2 * r + u
                        step.turn(act3, t, 1)
                        inverse(t, u)
                        if u == 0 and (r == 0 or not isinstance(s, int) or s < NC - 1):
                            block_weights(s + r, 1 - r)
                        if not isinstance(t, int) or t >= 1:
                            logs(t - 1, 1 - u)

            act3 = step.n
            block_weights(0, 0)
            units(0)
            with act.Fori(1, NC - 1) as s:
                units(s)
            units(NC - 1)
            logs(UNITS - 1, 1)

            def copy_feat(c, q, n):
                act.wait_ge(pair_turned, n + c + 1)
                act.activation(featT[:, q, :], (tp, ux_bank)[q][0:D, 0:CW], ACT.Copy).then_inc(feat_ready, 1)

            each_pair(act, lambda c, q: copy_feat(c, q, 0))
            root(3 * NC + 1, pn[:, 6, :], pn[:, 5, :])
            act.wait_ge(nv_ready, 1)
            act.activation(pn[:, 7, :], pn[:, 6, :], ACT.Tanh).then_inc(tanh3_ready, 1)
            root(3 * NC + 2, pn[:, 2, :], pn[:, 1, :])
            for k in range(0, NB, 4):
                n = min(4, NB - k) * P
                act.wait_ge(counts_turned, k // 4 + 1)
                act.activation(countsT[:, k * P:k * P + n], agg[0:NB, k // 4 % 2, 0:n], ACT.Copy) \
                    .then_inc(counts_copied, 1)
            each_pair(act, lambda c, q: copy_feat(c, q, NC))

            def weights(c, q):
                for g, (j, n) in enumerate(GROUP):
                    if g % 2 == 0:
                        act.wait_ge(exps_made[0], GROUPS[0] * c + g // 2 + 1)
                        if g == 0 and (not isinstance(c, int) or c >= 2):
                            act.wait_ge(agg_ready, 2 * NC + c - 1)
                        act.activation(w_exp[q][:, j:j + n, :].rearrange("p j n -> p (j n)"),
                                       exp_ps[0][:, 0:n * CW], ACT.Relu, bias=W_SHIFT) \
                            .then_inc(exps_read[0], 1)

            each_pair(act, weights)

        @block.tensor
        def _(pe):
            pe.wait_ge(weights_loaded, 160)
            pe.wait_ge(consts_made, 2)
            pe.wait_ge(rows_made, 2)
            pe.matmul(one[:, 0:1], t_rows, t_one[:, :], start=True, stop=True).then_inc(bias_ps_ready, 1)

            def turn_pair(src, n):
                pe.wait_ge(h_ready, n + 1)
                if not isinstance(n, int) or n >= 1:
                    pe.wait_ge(hT_ready, n)
                pe.matmul(tp[0:D, 0:P], src[:, 0, :], ident[:, :], start=True, stop=True)
                pe.matmul(tp[0:D, P:CW], src[:, 1, :], ident[:, :], start=True, stop=True).then_inc(turned, 1)

            def products0(c, q):
                turn_pair(h_pair[:, q], c)
                pe.wait_ge(hT_ready, c + 1)
                if not isinstance(c, int) or c >= 2:
                    pe.wait_ge(z_split, c - 1)
                for b in range(2):
                    ins = pe.matmul((mm, one)[q][:, b * P:(b + 1) * P], hT[:, b * P:(b + 1) * P], w0[:, :],
                                    start=True, stop=True)
                ins.then_inc(z_ready, 1)

            pe.wait_ge(bias_ready, 1)
            products0(0, 0)
            products0(1, 1)
            with pe.Fori(2, NC - 1, 2) as c:
                products0(c, 0)
                products0(c + 1, 1)
            products0(NC - 1, 0)

            def gather(c, q, n, terms, width):
                if not isinstance(n, int) or n >= 2:
                    pe.wait_ge(agg_read, n - 1)
                for b in range(2):
                    for j in range(NB):
                        ins = pe.matmul(agg[:, 2 * q + b, 0:width],
                                        adj[:, c, j * CW + b * P:j * CW + (b + 1) * P],
                                        terms[:, j, 0:width], start=(j == 0), stop=(j == NB - 1))
                ins.then_inc(agg_ready, 1)

            def products1(c):
                turn_pair(t_c, NC + c)
                pe.wait_ge(hT_ready, NC + c + 1)
                if not isinstance(c, int) or c >= 1:
                    pe.wait_ge(base_ready, c)
                    pe.wait_ge(tanh_ready, c)
                pe.matmul(mm[:, 0:CW], w1h[:, :], hT[0:D, :], start=True, stop=True).then_inc(hid_ready, 1)
                for b in range(2):
                    pe.matmul(ux[:, b, 0:D], hT[0:D, b * P:(b + 1) * P], w1b[:, :], start=True, stop=True)
                pe.wait_ge(tanh_ready, c + 1)
                for b in range(2):
                    pe.matmul(ux[:, b, D:2 * D], hidT[:, b * P:(b + 1) * P], w1o[:, :], start=True, stop=False)
                    ins = pe.matmul(ux[:, b, D:2 * D], ones_row[:, :], b1o[:, :], start=False, stop=True)
                ins.then_inc(ux_ready, 1)

            def layer1(c, q):
                pe.wait_ge(adj_loaded[q], (c // 2 + 1) * 16)
                gather(c, q, c, z_spl, SPL + NB)
                if not isinstance(c, int) or c >= 1:
                    products1(c - 1)

            pe.wait_ge(z_split, NC)
            layer1(0, 0)
            layer1(1, 1)
            with pe.Fori(2, NC - 1, 2) as c:
                layer1(c, 0)
                layer1(c + 1, 1)
            layer1(NC - 1, 0)
            products1(NC - 1)
            pe.wait_ge(base_ready, NC)

            with pe.Fori(0, NC - 1, 2) as c:
                gather(c, 1, NC + c, xb_spl, SPL)
                gather(c + 1, 0, NC + c + 1, xb_spl, SPL)
            gather(NC - 1, 1, 2 * NC - 1, xb_spl, SPL)


            pe.wait_ge(late_made, 2)

            def augment(c, q):
                pe.wait_ge(aug_made, c + 1)
                if not isinstance(c, int) or c >= 2:
                    pe.wait_ge(row_copied, c - 1)
                for b in range(2):
                    pe.transpose(aug_ps[q][0:K2, b * P:(b + 1) * P], aug_l[:, q, b, :], ident[:, :])
                for b in range(2):
                    ins = pe.transpose(aug_ps[q][0:K2, CW + b * P:CW + (b + 1) * P], aug_r[:, q, b, :],
                                       ident[:, :])
                ins.then_inc(aug_turned, 1)
                pe.wait_ge(aug_copied, c + 1)
                pe.matmul(row_ps[q][:, 0:CW], pick_b[:, :], rhs_aug[:, bass.ds(c * CW, CW)],
                          start=True, stop=True).then_inc(row_ready, 1)

            each_pair(pe, augment)
            pe.wait_ge(wrapped, 3)
            for b in range(4):
                pe.matmul(agg[:, b, :], ones_row[:, :], zero_row[:, :], start=True, stop=False,
                          skip_group_check=True)

            def distances(s, r, u):
                t = 4 * s + 2 * r + u
                if u == 0:
                    pe.wait_ge(lhs_copied, 2 * s + r + 1)
                if not isinstance(t, int) or t >= 1:
                    pe.wait_ge(apart, t)
                for at in range(0, UW[u], 512):
                    n = min(512, UW[u] - at)
                    ins = pe.matmul(dist_ps[:, at:at + n], lhs_one[:, r, :],
                                    rhs_aug[:, bass.ds(s * CW + UO[u] * P + at, n)], start=True, stop=True)
                ins.then_inc(dist_ready, 1)

            def sums(s, r, u):
                t = 4 * s + 2 * r + u
                pe.wait_ge(gain_ready, t + 1)
                for h in range(2):
                    if not isinstance(t, int) or t >= 1:
                        pe.wait_ge(tr_ready, 2 * t - 1 + h)
                    for k in range(3):
                        at = (UT[u] - UO[u] + 3 * h + k) * P
                        ins = pe.transpose(turn_ps[:, h, k * P:(k + 1) * P], gain[u][:, at:at + P], ident[:, :])
                    ins.then_inc(turn_ready, 1)
                pe.wait_ge(dir_ready, t + 1)
                for k in range(UB[u]):
                    j = (2 * s + UO[u] + k) % NB
                    ins = pe.matmul(lo[:, bass.ds(acc_at(j), NW)], p_dir[u][:, k * P:(k + 1) * P],
                                    xrow[:, 2 * s + r, :], start=False, stop=False, skip_group_check=True)
                ins.then_inc(dir_used, 1)
                for h in range(2):
                    pe.wait_ge(tr_ready, 2 * t + 1 + h)
                    for k in range(3):
                        m = 3 * h + k
                        ins = pe.matmul(lo[:, bass.ds(acc_at(2 * s + r), NW)], p_tr[u][:, m * P:(m + 1) * P],
                                        xrow[:, 2 * s + UT[u] + m, :], start=False, stop=False,
                                        skip_group_check=True)
                ins.then_inc(tr_used, 1)

            def units(s):
                for r in range(2):
                    for u in range(2):
                        last = isinstance(s, int) and s == NC - 1 and r == 1 and u == 1
                        if not last:
                            k = 2 * r + u + 1
                            distances(s + k // 4, k // 2 % 2, k % 2)
                        if r == 1:
                            sums(s, 0, u)
                        elif not isinstance(s, int) or s >= 1:
                            sums(s - 1, 1, u)

            distances(0, 0, 0)
            units(0)
            with pe.Fori(1, NC - 1) as s:
                units(s)
            units(NC - 1)
            sums(NC - 1, 1, 0)
            sums(NC - 1, 1, 1)
            pe.wait_ge(late_loaded, 64)

            def linear(c, q, n, w, bias):
                pe.wait_ge(pair_ready, n + c + 1)
                pe.matmul((tp, ux_bank)[q][0:D, 0:P], row_pair[:, q, 0, :], ident[:, :], start=True, stop=True)
                pe.matmul((tp, ux_bank)[q][0:D, P:CW], row_pair[:, q, 1, :], ident[:, :], start=True, stop=True) \
                    .then_inc(pair_turned, 1)
                pe.wait_ge(feat_ready, n + c + 1)
                if n or not isinstance(c, int) or c >= 2:
                    pe.wait_ge(lin_read, n + c - 1)
                for b in range(2):
                    dst = (mm, one)[q][:, b * P:b * P + D]
                    ins = pe.matmul(dst, featT[:, q, b * P:(b + 1) * P], w[:, :], start=True, stop=bias is None)
                    if bias is not None:
                        ins = pe.matmul(dst, ones_row[:, :], bias[:, :], start=False, stop=True)
                ins.then_inc(lin_ready, 1)

            each_pair(pe, lambda c, q: linear(c, q, 0, w2h, b2h))
            for k in range(0, NB, 4):
                if k >= 8:
                    pe.wait_ge(counts_copied, k // 4 - 1)
                for m in range(min(4, NB - k)):
                    ins = pe.matmul(agg[0:NB, k // 4 % 2, m * P:(m + 1) * P], counts[:, k + m, :],
                                    ident16[:, :], start=True, stop=True)
                ins.then_inc(counts_turned, 1)
            each_pair(pe, lambda c, q: linear(c, q, NC, w3d, None))
            pe.wait_ge(lin_read, 2 * NC)
            pe.wait_ge(counts_copied, (NB + 3) // 4)
            pe.wait_ge(late_made, 3)

            def exponents(c, q):
                pe.wait_ge(adj4_loaded[q], (c // 2 + 1) * 16)
                for g, (j, n) in enumerate(GROUP):
                    k = g % 2
                    if g >= 2 or not isinstance(c, int) or c >= 1:
                        pe.wait_ge(exps_read[k], GROUPS[k] * c + g // 2)
                    for m in range(n):
                        dst = exp_ps[k][:, m * CW:(m + 1) * CW]
                        pe.matmul(dst, order[:, :], adj4[q][:, (j + m) * CW:(j + m + 1) * CW],
                                  start=True, stop=False)
                        ins = pe.matmul(dst, later[:, j + m, :], countsT[:, bass.ds(c * CW, CW)],
                                        start=False, stop=True)
                    ins.then_inc(exps_made[k], 1)

            def decayed(c, q):
                for k in range(2):
                    pe.wait_ge(exps_read[k], GROUPS[k] * (c + 1))
                if not isinstance(c, int) or c >= 2:
                    pe.wait_ge(agg_read, 2 * NC + c - 1)
                for b in range(2):
                    for j in range(NB):
                        ins = pe.matmul(agg[:, 2 * q + b, 0:SPL],
                                        w_exp[q][:, j, b * P:(b + 1) * P].bitcast(bf16),
                                        s_spl[:, j, :], start=(j == 0), stop=(j == NB - 1))
                ins.then_inc(agg_ready, 1)

            def layer4(c, q):
                exponents(c, q)
                if not isinstance(c, int) or c >= 1:
                    decayed(c - 1, 1 - q)

            each_pair(pe, layer4)
            decayed(NC - 1, 0)

        @block.vector
        def _(dve):
            step = Chain(dve, dve_step)
            s = [small[:, k, :] for k in range(16)]

            def root(n):
                dve.wait_ge(root_ready, n + 1)

            dve.memset(hT[D:NW, :], 1.0).then_inc(rows_made, 1)
            dve.memset(w0[D:NW, D:2 * D], 0.0).then_inc(rows_made, 1)
            dve.wait_ge(x_all_loaded, 16)
            sa = [st_all[:, k, :] for k in range(4)]
            step(dve.tensor_reduce(sa[0], x_all[:, :, :], AX, ALU.add))
            step(dve.tensor_scalar(sa[0], sa[0], -1.0 / D, None, ALU.mult))
            step(dve.tensor_tensor(x_all[:, :, :], x_all[:, :, :], wide(sa[0]), ALU.add))
            step(dve.tensor_tensor(sq_all[:, :, :], x_all[:, :, :], x_all[:, :, :], ALU.mult))
            step(dve.tensor_reduce(sa[1], sq_all[:, :, :], AX, ALU.add))
            dve.tensor_scalar(sa[1], sa[1], 1.0 / D, EPS, ALU.mult, ALU.add).then_inc(var_ready, 1)
            root(0)
            step(dve.reciprocal(sa[3], sa[2]))

            def norm0(c, q):
                if not isinstance(c, int) or c >= 2:
                    dve.wait_ge(turned, c - 1)
                dve.scalar_tensor_tensor(h_pair[:, q], pair(x_all, c), 0.0, wide(sa[3][:, bass.ds(2 * c, 2)]),
                                         ALU.max, ALU.mult).then_inc(h_ready, 1)

            def split(chain, dst, v, n, last=None):
                chain(dve.tensor_copy(dst[:, :, 0:D], v))
                chain(dve.tensor_tensor(t_b[:, :, :], v, dst[:, :, 0:D], ALU.subtract))
                chain(dve.tensor_copy(dst[:, :, D:2 * D], t_b[:, :, :]))
                ins = dve.tensor_tensor(dst[:, :, 2 * D:SPL], t_b[:, :, :], dst[:, :, D:2 * D], ALU.subtract)
                chain(ins) if last is None else ins.then_inc(last, 1)

            def split0(c, q):
                step.turn(start, c, 4)
                dve.wait_ge(z_ready, c + 1)
                m = (mm, one)[q][:, 0:CW].rearrange("p (b n) -> p b n", b=2)
                step(dve.tensor_copy(pair(base, c), m[:, :, 0:D]))
                split(step, pair(z_spl, c), m[:, :, D:2 * D], c, z_split)

            start = step.n
            norm0(0, 0)
            norm0(1, 1)
            with dve.Fori(0, NC - 3, 2) as c:
                split0(c, 0)
                norm0(c + 2, 0)
                split0(c + 1, 1)
                norm0(c + 3, 1)
            split0(NC - 3, 0)
            norm0(NC - 1, 0)
            split0(NC - 2, 1)
            split0(NC - 1, 0)

            def layer_norm(v, h, n, event):
                step(dve.tensor_reduce(s[7], v, AX, ALU.add))
                step(dve.tensor_scalar(s[7], s[7], -1.0 / D, None, ALU.mult))
                step(dve.tensor_tensor(t_b[:, :, :], v, wide(s[7]), ALU.add))
                step(dve.tensor_tensor(t_c[:, :, :], t_b[:, :, :], t_b[:, :, :], ALU.mult))
                step(dve.tensor_reduce(s[8], t_c[:, :, :], AX, ALU.add))
                dve.tensor_scalar(s[8], s[8], 1.0 / D, EPS, ALU.mult, ALU.add).then_inc(var_ready, 1)
                root(n)
                step(dve.reciprocal(s[10], s[9]))
                dve.scalar_tensor_tensor(h, t_b[:, :, :], 0.0, wide(s[10]), ALU.max, ALU.mult) \
                    .then_inc(event, 1)

            def sum_parts(v):
                return v.rearrange("p b (k d) -> p b d k", k=3)

            def layer12(c, q):
                step.turn(start1, c, STEPS1)
                dve.wait_ge(agg_ready, c + 1)
                got = agg[:, 2 * q:2 * q + 2, :]
                step(dve.tensor_tensor(rows[:, :, :], got[:, :, 0:SPL], pair(z_spl, c)[:, :, 0:SPL], ALU.add))
                step(dve.tensor_copy(pair(counts, c), got[:, :, SPL:SPL + NB]))
                dve.tensor_reduce(s[0], got[:, :, SPL:SPL + NB], AX, ALU.add).then_inc(agg_read, 1)
                dve.wait_ge(agg_read, c + 1)
                step(dve.tensor_reduce(t_a[:, :, :], sum_parts(rows[:, :, :]), AX, ALU.add))
                step(dve.tensor_scalar(deg[:, bass.ds(2 * c, 2)], s[0], 0.0, None, ALU.add))
                step(dve.tensor_scalar(s[1], s[0], 1.0, 1.0, ALU.add, ALU.max))
                step(dve.reciprocal(s[2], s[1]))
                step(dve.tensor_tensor(t_a[:, :, :], t_a[:, :, :], wide(s[2]), ALU.mult))
                step(dve.tensor_tensor(t_a[:, :, :], t_a[:, :, :], pair(base, c), ALU.add))
                step(dve.scalar_tensor_tensor(t_b[:, :, :], t_a[:, :, :], 0.0, t_a[:, :, :], ALU.max, ALU.mult))
                dve.tensor_reduce(s[3], t_b[:, :, :], AX, ALU.add).then_inc(var_ready, 1)
                root(2 * c + 1)
                step(dve.tensor_scalar(s[5], s[4], L2_EPS, None, ALU.max))
                step(dve.reciprocal(s[6], s[5]))
                step(dve.scalar_tensor_tensor(t_b[:, :, :], t_a[:, :, :], 0.0, wide(s[6]), ALU.max, ALU.mult))
                dve.wait_ge(x_in_sem[q], (c // 2 + 1) * 16)
                step(dve.tensor_tensor(t_a[:, :, :], t_b[:, :, :], x_in[:, q], ALU.add))
                layer_norm(t_a[:, :, :], t_c[:, :, :], 2 * c + 2, h_ready)
                dve.wait_ge(ux_ready, c + 1)
                step(dve.tensor_copy(xb[:, :, :], ux[:, :, 0:D]))
                split(step, pair(xb_spl, c), xb[:, :, :], c)
                step(dve.tensor_tensor(t_b[:, :, :], xb[:, :, :], wide(s[0]), ALU.mult))
                step(dve.tensor_tensor(t_a[:, :, :], t_a[:, :, :], t_b[:, :, :], ALU.subtract))
                dve.tensor_tensor(pair(base, c), t_a[:, :, :], ux[:, :, D:2 * D], ALU.add).then_inc(base_ready, 1)
                assert step.n == STEPS1, step.n

            start1 = start + 4 * NC
            each_pair(dve, layer12)

            def layer2(c, q):
                step.turn(start2, c, STEPS2)
                dve.wait_ge(agg_ready, NC + c + 1)
                dve.tensor_reduce(t_a[:, :, :], sum_parts(agg[:, 2 * q:2 * q + 2, 0:SPL]), AX, ALU.add) \
                    .then_inc(agg_read, 1)
                dve.wait_ge(agg_read, NC + c + 1)
                step(dve.tensor_tensor(t_a[:, :, :], t_a[:, :, :], pair(base, c), ALU.add))
                dve.tensor_scalar(pair(base, c), t_a[:, :, :], 0.0, None, ALU.add).then_inc(x2_ready, 1)
                layer_norm(t_a[:, :, :], pair(h2, c), 2 * NC + 1 + c, h2_ready)
                assert step.n == STEPS2, step.n

            start2 = start1 + STEPS1 * NC
            with dve.Fori(0, NC - 1, 2) as c:
                layer2(c, 1)
                layer2(c + 1, 0)
            layer2(NC - 1, 1)
            print("steps", start, start1, start2)

            start3 = start2 + STEPS2 * NC
            step.turn(start3, 0, 0)
            dve.wait_ge(h2_ready, NC)
            sq = post[1][:, :, :]
            step(dve.tensor_tensor(sq, h2[:, :, :], h2[:, :, :], ALU.mult))
            step(dve.tensor_reduce(x2[:, :], sq, AX, ALU.add))
            step(dve.memset(zero_row[:, :], 0.0))
            for q in range(2):
                step(dve.memset(aug_l[:, q, :, D + 1:K2], 1.0))
                step(dve.memset(aug_r[:, q, :, D:D + 1], 1.0))

            def augment(c, q):
                step.turn(start3 + 7, c, 3)
                if not isinstance(c, int) or c >= 2:
                    dve.wait_ge(aug_turned, c - 1)
                norms = x2[:, bass.ds(2 * c, 2)].unsqueeze(2)
                step(dve.tensor_scalar(aug_l[:, q, :, 0:D], pair(h2, c), 1.0, None, ALU.mult))
                step(dve.tensor_scalar(aug_r[:, q, :, 0:D], pair(h2, c), -2.0, None, ALU.mult))
                step(dve.tensor_scalar(aug_l[:, q, :, D:D + 1], norms, 1.0, None, ALU.mult))
                dve.tensor_scalar(aug_r[:, q, :, D + 1:K2], norms, 1.0, None, ALU.mult).then_inc(aug_made, 1)

            each_pair(dve, augment)
            start3 += 7 + 3 * NC
            step.turn(start3, 0, 0)
            step(dve.tensor_scalar(x_b[:, :], x2[:, :], -1.0, 1.0, ALU.mult, ALU.add))
            step(dve.tensor_copy(xrow[:, 0:NB, 0:D], h2[:, :, :]))
            step(dve.tensor_scalar(xrow[:, 0:NB, D:NW], x2[:, :].unsqueeze(2), 1.0, None, ALU.add))
            dve.tensor_copy(xrow[:, NB:EXB, :], xrow[:, 0:EXB - NB, :]).then_inc(wrapped, 1)
            dve.wait_ge(row_copied, NC)
            dve.tensor_copy(rhs_aug[:, NP:EXB * P], rhs_aug[:, 0:EXB * P - NP]).then_inc(wrapped, 1)
            dve.tensor_copy(x_b_row[:, NP:EXB * P], x_b_row[:, 0:EXB * P - NP]).then_inc(wrapped, 1)
            dve.wait_ge(wrapped, 3)

            def front(s, r, u):
                t = 4 * s + 2 * r + u
                if not isinstance(t, int) or t >= 1:
                    dve.wait_ge(prod_ready, t)
                dve.wait_ge(dist_ready, t + 1)
                d, w = den[:, 0:UW[u]], dist_ps[:, 0:UW[u]]
                step(dve.scalar_tensor_tensor(d, x_b_row[:, bass.ds(s * CW + UO[u] * P, UW[u])],
                                              x_b[:, bass.ds(2 * s + r, 1)], w, ALU.mult, ALU.add))
                step(dve.tensor_scalar(d, d, MIN_NORM, None, ALU.max))
                dve.scalar_tensor_tensor(dist[u][:, :], d, NORM_FLOOR, w, ALU.mult, ALU.max).then_inc(apart, 1)

            def middle(t, u):
                dve.wait_ge(inv_ready, t + 1)
                step(dve.tensor_tensor(nrm[u][:, :], dist[u][:, :], inv[u][:, :], ALU.mult))
                dve.tensor_scalar(nrm[u][:, :], nrm[u][:, :], TANH_CLIP, None, ALU.min).then_inc(nrm_ready, 1)

            def back(s, r, u):
                t = 4 * s + 2 * r + u
                dve.wait_ge(atanh_ready, t + 1)
                dve.scalar_tensor_tensor(gain[u][:, :], gain[u][:, :], 0.5, inv[u][:, :], ALU.mult, ALU.mult) \
                    .then_inc(gain_ready, 1)
                dve.wait_ge(gain_ready, t + 1)
                dve.wait_ge(mask_loaded[u][r], 16 * s + 16)
                if not isinstance(t, int) or t >= 2:
                    dve.wait_ge(dir_used, t - 1)
                dve.tensor_tensor(p_dir[u][:, :], gain[u][:, :], mask[u][r][:, 0:UW[u]], ALU.mult) \
                    .then_inc(dir_ready, 1)
                if not isinstance(t, int) or t >= 2:
                    dve.wait_ge(tr_used, t - 1)
                for h in range(2):
                    dve.wait_ge(turn_ready, 2 * t + h + 1)
                    dve.tensor_tensor(p_tr[u][:, 3 * h * P:3 * (h + 1) * P], turn_ps[:, h, 0:3 * P],
                                      mask[u][r][:, UW[u] + 3 * h * P:UW[u] + 3 * (h + 1) * P], ALU.mult) \
                        .then_inc(tr_ready, 1)

            def units(s):
                for r in range(2):
                    for u in range(2):
                        k = 2 * r + u
                        step.turn(start3, 4 * s + k, 3)
                        front(s, r, u)
                        if k >= 1 or not isinstance(s, int) or s >= 1:
                            middle(4 * s + k - 1, 1 - u)
                        else:
                            step.eng.wait_ge(apart, 1)
                            step(dve.tensor_copy(s16, s16b))
                        if k >= 2:
                            back(s, 0, u)
                        elif not isinstance(s, int) or s >= 1:
                            back(s - 1, 1, u)

            start3 += step.n
            s16, s16b = small[:, 14, :], small[:, 15, :]
            step.turn(start3, 0, 0)
            step(dve.memset(s16b, 0.0))
            start3 += 1
            units(0)
            with dve.Fori(1, NC) as s:
                units(s)
            start3 += 3 * UNITS
            step.turn(start3, 0, 0)
            middle(UNITS - 1, 1)
            back(NC - 1, 1, 0)
            back(NC - 1, 1, 1)

            dve.wait_ge(tr_used, UNITS)
            u_sum, tmp, lin = post[0], post[1], post[2]
            p = [pn[:, k, :] for k in range(8)]
            for b in range(4):
                n = min(7, NB - 7 * b)
                got = agg[:, b, 0:504].rearrange("p (k n) -> p k n", k=7)[:, 0:n]
                step(dve.tensor_copy(u_sum[:, 7 * b:7 * b + n, :], got[:, :, 0:D]))
                step(dve.tensor_copy(pn[:, 0, 7 * b:7 * b + n].unsqueeze(2), got[:, :, D:NW]))
            step(dve.tensor_tensor(tmp[:, :, :], u_sum[:, :, :], h2[:, :, :], ALU.mult))
            step(dve.tensor_reduce(p[1], tmp[:, :, :], AX, ALU.add))
            step(dve.scalar_tensor_tensor(p[2], p[1], -2.0, p[0], ALU.mult, ALU.add))
            step(dve.tensor_tensor(tmp[:, :, :], h2[:, :, :], wide(p[2]), ALU.mult))
            step(dve.tensor_tensor(u_sum[:, :, :], u_sum[:, :, :], wide(x_b[:, :]), ALU.mult))
            step(dve.tensor_tensor(u_sum[:, :, :], u_sum[:, :, :], tmp[:, :, :], ALU.subtract))
            step(dve.tensor_scalar(p[3], deg[:, :], 1e-8, None, ALU.max))
            step(dve.reciprocal(p[4], p[3]))
            step(dve.tensor_scalar(p[3], x_b[:, :], MIN_NORM, None, ALU.max))
            step(dve.tensor_tensor(p[3], p[3], p[4], ALU.mult))

            def rows_out(c, q, n, v, scale, op0):
                if n or not isinstance(c, int) or c >= 2:
                    dve.wait_ge(pair_turned, n + c - 1)
                dve.scalar_tensor_tensor(row_pair[:, q], pair(v, c), 0.0 if op0 == ALU.max else 1.0,
                                         wide(scale[:, bass.ds(2 * c, 2)]), op0, ALU.mult).then_inc(pair_ready, 1)

            def take(c, q):
                dve.wait_ge(lin_ready, c + 1)
                got = (mm, one)[q][:, 0:CW].rearrange("p (b n) -> p b n", b=2)[:, :, 0:D]
                dve.tensor_scalar(pair(lin, c), got, 1.0, None, ALU.mult).then_inc(lin_read, 1)

            def ahead(out_of, into):
                out_of(0, 0)
                out_of(1, 1)
                with dve.Fori(0, NC - 3, 2) as c:
                    into(c, 0)
                    out_of(c + 2, 0)
                    into(c + 1, 1)
                    out_of(c + 3, 1)
                into(NC - 3, 0)
                out_of(NC - 1, 0)
                into(NC - 2, 1)
                into(NC - 1, 0)

            ahead(lambda c, q: rows_out(c, q, 0, u_sum, p[3], ALU.mult), take)
            dve.wait_ge(lin_read, NC)
            step(dve.tensor_tensor(tmp[:, :, :], lin[:, :, :], lin[:, :, :], ALU.mult))
            dve.tensor_reduce(p[5], tmp[:, :, :], AX, ALU.add).then_inc(var_ready, 1)
            root(3 * NC + 1)
            dve.tensor_scalar(p[6], p[6], MIN_NORM, None, ALU.max).then_inc(nv_ready, 1)
            dve.wait_ge(nv_ready, 1)
            step(dve.reciprocal(p[5], p[6]))
            dve.wait_ge(tanh3_ready, 1)
            step(dve.tensor_tensor(p[7], p[7], p[5], ALU.mult))
            step(dve.tensor_tensor(lin[:, :, :], lin[:, :, :], wide(p[7]), ALU.mult))
            dve.tensor_tensor(base[:, :, :], base[:, :, :], lin[:, :, :], ALU.add).then_inc(x3_ready, 1)
            dve.wait_ge(x3_ready, 1)

            hc, sq4 = post[0], post[1]
            step(dve.tensor_reduce(p[0], base[:, :, :], AX, ALU.add))
            step(dve.tensor_scalar(p[0], p[0], -1.0 / D, None, ALU.mult))
            step(dve.tensor_tensor(hc[:, :, :], base[:, :, :], wide(p[0]), ALU.add))
            step(dve.tensor_tensor(sq4[:, :, :], hc[:, :, :], hc[:, :, :], ALU.mult))
            step(dve.tensor_reduce(p[3], sq4[:, :, :], AX, ALU.add))
            dve.tensor_scalar(p[1], p[3], 1.0 / D, EPS, ALU.mult, ALU.add).then_inc(var_ready, 1)
            step(dve.tensor_tensor(base[:, :, :], base[:, :, :],
                                   b3_all[:, :].unsqueeze(1).broadcast_to([P, NB, D]), ALU.add))
            root(3 * NC + 2)
            step(dve.reciprocal(p[3], p[2]))
            start4 = start3 + step.n

            def split4(c, q):
                step.turn(start4, c, 3)
                dve.wait_ge(lin_ready, NC + c + 1)
                got = (mm, one)[q][:, 0:CW].rearrange("p (b n) -> p b n", b=2)[:, :, 0:D]
                split(step, pair(s_spl, c), got, c, lin_read)

            ahead(lambda c, q: rows_out(c, q, NC, hc, p[3], ALU.max), split4)
            start4 += 3 * NC

            def layer4(c, q):
                for g, (j, n) in enumerate(GROUP):
                    if g % 2 == 1:
                        dve.wait_ge(exps_made[1], GROUPS[1] * c + g // 2 + 1)
                        if g == 1 and (not isinstance(c, int) or c >= 2):
                            dve.wait_ge(agg_ready, 2 * NC + c - 1)
                        dve.tensor_scalar(w_exp[q][:, j:j + n, :].rearrange("p j n -> p (j n)"),
                                          exp_ps[1][:, 0:n * CW], W_SHIFT, 0.0, ALU.add, ALU.max) \
                            .then_inc(exps_read[1], 1)

            def result(c, q):
                step.turn(start4, c, 1)
                dve.wait_ge(agg_ready, 2 * NC + c + 1)
                dve.tensor_reduce(t_a[:, :, :], sum_parts(agg[:, 2 * q:2 * q + 2, 0:SPL]), AX, ALU.add) \
                    .then_inc(agg_read, 1)
                dve.wait_ge(agg_read, 2 * NC + c + 1)
                if not isinstance(c, int) or c >= 2:
                    dve.wait_ge(out_sent[q], c // 2 * 16)
                step(dve.tensor_scalar(t_a[:, :, :], t_a[:, :, :], 2.0 ** (127 - HORIZON), None, ALU.mult))
                dve.tensor_tensor(o_buf[:, q], t_a[:, :, :], pair(base, c), ALU.add).then_inc(out_made, 1)
                dve.wait_ge(out_made, c + 1)

            def both(c, q):
                layer4(c, q)
                if not isinstance(c, int) or c >= 2:
                    result(c - 2, q)

            dve.wait_ge(lin_read, 2 * NC)
            each_pair(dve, both)
            result(NC - 2, 1)
            result(NC - 1, 0)


def kernel(x, adj, L0_gnn_W, L0_gnn_b, L1_gnn_t, L1_gnn_B, L1_gnn_W1, L1_gnn_b1, L1_gnn_W2, L1_gnn_b2,
           L2_gnn_weight, L2_gnn_bias, L3_gnn_weight, L3_gnn_bias):
    import numpy as np
    import concourse.bacc as bacc
    from concourse.bass_utils import run_bass_kernel_spmd

    x, adj = np.asarray(x), np.asarray(adj)
    rows = np.zeros((NP, D), x.dtype)
    rows[:N] = x
    rows = rows.reshape(NB, P, D).transpose(1, 0, 2)
    turned = np.zeros((NP, NP), adj.dtype)
    turned[:N, :N] = adj.T
    cols = turned.reshape(NB, P, NC, CW).transpose(2, 1, 0, 3).reshape(NC, P, NB * CW)
    tiles = turned.reshape(NB, P, NB, P)
    mask = np.empty((NB, P, NB, P), adj.dtype)
    for i in range(NB):
        first = i // 2 * 2
        at = 0
        for u in range(2):
            for k in range(UO[u], UO[u] + UB[u]):
                mask[i, :, at] = tiles[i, :, (first + k) % NB]
                at += 1
            for k in range(UT[u], UT[u] + 6):
                mask[i, :, at] = tiles[(first + k) % NB, :, i]
                at += 1
    w0, w1 = np.asarray(L0_gnn_W), np.asarray(L1_gnn_W1)
    laid = dict(x=rows, adj_cols=cols, adj_mask=mask.reshape(NB, P, NP),
                w_self=w0[:D], w_neigh=w0[D:], b0=np.asarray(L0_gnn_b).reshape(1, D),
                t1=np.stack([np.asarray(L1_gnn_t), np.ones_like(L1_gnn_t)]), bt1=np.asarray(L1_gnn_B).T, w11=w1,
                b11=np.asarray(L1_gnn_b1).reshape(1, HID), w12=np.asarray(L1_gnn_W2),
                b12=np.asarray(L1_gnn_b2).reshape(1, D),
                w_hyp=np.asarray(L2_gnn_weight), b_hyp=np.asarray(L2_gnn_bias).reshape(1, D),
                w_dec=np.asarray(L3_gnn_weight), b_dec=np.asarray(L3_gnn_bias).reshape(1, D))
    nc = bacc.Bacc("TRN2", target_bir_lowering=False, num_devices=1)
    arrays, args = {}, []
    for name, a in laid.items():
        arrays[f"in_{name}"] = np.ascontiguousarray(a)
        args.append(nc.dram_tensor(f"in_{name}", a.shape, mybir.dt.from_np(a.dtype), kind="ExternalInput").ap())
    args.append(nc.dram_tensor("out_rows", (P, NB, D), mybir.dt.float32, kind="ExternalOutput").ap())
    gnn_stack(nc, *args)
    got = run_bass_kernel_spmd(nc, [arrays], core_ids=[0]).results[0]["out_rows"]
    return np.ascontiguousarray(np.asarray(got).transpose(1, 0, 2).reshape(NP, D)[:N])
```

```python
import concourse.bass as bass
from concourse import mybir
from contextlib import ExitStack

N = 3327
D = 64
HID = 128
P = 128
NB = 26
NP = NB * P
NC = NB // 2
CW = 2 * P
TURNS = 7
KN = 6
NW = D + 1
SPL = 3 * D
EXB = 38
UB = (8, 6)
UO = (0, 8)
UT = (2, 8)
HORIZON = 100
EDGE = 16384.0
MIN_NORM = 1e-15
LN_FLOOR = 2.0 ** -63
TANH_CLIP = 1.0 - 168 * 2.0 ** -24
EPS = 1e-05
L2_EPS = 1e-12
NORM_FLOOR = 2.0 ** -22


def gnn_stack(nc, x, adj_cols, adj_mask, w_self, w_neigh, b0, t1, bt1, w11, b11, w12, b12,
              w_hyp, b_hyp, w_dec, b_dec, out):
    fp32, bf16, i16 = mybir.dt.float32, mybir.dt.bfloat16, mybir.dt.int16
    ALU, ACT = mybir.AluOpType, mybir.ActivationFunctionType
    AX = mybir.AxisListType.X
    ctx = ExitStack()
    with ctx:
        cursor = [(nc.sbuf_base + 63) // 64 * 64]

        def place(name, shape, dt=fp32):
            n = 1
            for s in shape[1:]:
                n *= s
            at = cursor[0]
            cursor[0] = at + (n * mybir.dt.size(dt) + 31) // 32 * 32
            return nc.alloc_sbuf_tensor_at(name, shape, dt, offset=at)

        def sem(name):
            return ctx.enter_context(nc.semaphore(name))

        ident = place("ident", [P, P])
        counts = place("counts", [P, NB, NB], bf16)
        deg = place("deg", [P, NB])
        base = place("base", [P, NB, D])
        small = place("small", [P, 16, 2])
        ones_row = place("ones_row", [1, P])
        rows = place("rows", [P, 2, SPL])
        t_a = place("t_a", [P, 2, D])
        t_b = place("t_b", [P, 2, D])
        t_c = place("t_c", [P, 2, D])
        kept = cursor[0]
        z_spl = place("z_spl", [P, NB, SPL + NB], bf16)
        w0 = place("w0", [NW, 2 * D])
        w1u = place("w1u", [NW, 2 * D])
        w1h = place("w1h", [D, HID])
        t_rows = rows[0:2, 0, 0:HID]
        t_one = place("t_one", [2, 1])
        bias11 = place("bias11", [HID, 1])
        w1o = place("w1o", [HID, D])
        x_in = place("x_in", [P, 2, 2, D])
        hT = place("hT", [NW, CW])
        hidT = place("hidT", [HID, CW])
        ux_in = place("ux_in", [P, 2, 2 * D])
        xb_spl = place("xb_spl", [P, NB, SPL], bf16)
        adj_at = cursor[0]
        adj = place("adj", [P, NC, NB * CW], bf16)
        cursor[0] -= 2 * NB * CW * mybir.dt.size(bf16)
        x_all = place("x_all", [P, NB, D])
        h_pair = place("h_pair", [P, 2, 2, D])
        sq_all = place("sq_all", [P, NB, D])
        st_all = place("st_all", [P, 4, NB])
        cursor[0] = kept
        h2 = place("h2", [P, NB, D])
        pick_b = place("pick_b", [KN, P], bf16)
        norms = place("norms", [P, NB, 10], bf16)
        w2h = place("w2h", [D, D])
        b2_all = place("b2_all", [P, D])
        w3d = place("w3d", [D, D])
        b3_all = place("b3_all", [P, D])
        zero_row = place("zero_row", [1, 512])
        ident16 = place("ident16", [P, P], bf16)
        order = place("order", [P, P], bf16)
        row_quad = place("row_quad", [P, 2, 4, D])
        featT = place("featT", [D, 2, 4 * P])
        t_quad = place("t_quad", [P, 4, D])
        x2 = place("x2", [P, NB])
        x_b = place("x_b", [P, NB])
        pn = place("pn", [P, 8, NB])
        late = cursor[0]
        assert late <= nc.sbuf_base + 63 + 40000
        parts = nc.alloc_sbuf_tensor_at("parts", [P, NB, TURNS * D], bf16, offset=adj_at)
        assert TURNS <= 8 and late <= adj_at
        UW = [n * P for n in UB]
        inv = [place(f"inv{k}", [P, UW[k % 2]]) for k in range(4)]
        nrm = [place(f"nrm{u}", [P, UW[u]]) for u in range(2)]
        gain = [place(f"gain{u}", [P, UW[u]]) for u in range(2)]
        den = place("den", [P, UW[0]])
        dist = [place(f"dist{k}", [P, UW[k]]) for k in range(2)]
        squares = place("squares", [P, NB, D])
        cursor[0] -= NB * D * 4
        p_dir = [place(f"p_dir{u}", [P, UW[u]]) for u in range(2)]
        p_tr = [place(f"p_tr{u}", [P, 6 * P]) for u in range(2)]
        xrow = place("xrow", [P, EXB, NW])
        own = place("own", [P, NB, 3, P], bf16)
        far12 = place("far12", [P, EXB * P], bf16)
        far31 = place("far31", [P, EXB * P], bf16)
        own_n = place("own_n", [KN, NP], bf16)
        far_n = place("far_n", [KN, EXB * P], bf16)
        x_b_row = place("x_b_row", [P, EXB * P])
        mask = [[place(f"mask{u}{k}", [P, UW[u] + 6 * P]) for k in range(2)] for u in range(2)]
        behind3 = cursor[0]
        adj4 = [place("adj4_0", [P, NB * CW], bf16)]
        assert cursor[0] <= nc.sbuf_usable_end, cursor
        cursor[0] = late
        adj4.append(place("adj4_1", [P, NB * CW], bf16))
        w_exp = [place(f"w_exp{k}", [P, NB, CW], i16) for k in range(2)]
        o_buf = place("o_buf", [P, 2, 2, D])
        s_spl = place("s_spl", [P, NB, SPL], bf16)
        countsT = place("countsT", [NB, NP], bf16)
        later = place("later", [NB, NB, P], bf16)
        post = [place(f"post{k}", [P, NB, D]) for k in range(4)]
        assert cursor[0] <= behind3

        lo = ctx.enter_context(nc.psum_tensor("lo", [P, 2048], fp32))
        hi = ctx.enter_context(nc.psum_tensor("hi", [P, 2048], fp32))
        agg = lo[:, :].rearrange("p (b n) -> p b n", b=4)
        tp = hi[:, 0:512]
        mm = hi[:, 512:1024]
        ux = hi[:, 1024:1536].rearrange("p (b n) -> p b n", b=2)
        one = hi[:, 1536:2048]
        ux_bank = hi[:, 1024:1536]
        side_ps = [b.rearrange("p (b k n) -> p b k n", b=2, k=2) for b in (tp, mm)]
        dist_ps = hi[:, 0:1024]
        turn_ps = hi[:, 1024:2048].rearrange("p (k n) -> p k n", k=2)
        exp_ps = [hi[:, 0:1024], hi[:, 1024:2048]]


        def acc_at(j):
            return j * 72 + j // 7 * 8

        x_in_sem = [sem(f"x_loaded{k}") for k in range(2)]
        x_all_loaded = sem("x_all_loaded")
        weights_loaded = sem("weights_loaded")
        adj_loaded = [sem(f"adj_loaded{k}") for k in range(2)]
        consts_made = sem("consts_made")
        dve_step = sem("dve_step")
        act_step = sem("act_step")
        pool_step = sem("pool_step")
        var_ready = sem("var_ready")
        root_ready = sem("root_ready")
        h_ready = sem("h_ready")
        turned = sem("turned")
        hT_ready = sem("hT_ready")
        z_ready = sem("z_ready")
        z_split = sem("z_split")
        agg_ready = sem("agg_ready")
        agg_read = sem("agg_read")
        hid_ready = sem("hid_ready")
        tanh_ready = sem("tanh_ready")
        ux_ready = sem("ux_ready")
        base_ready = sem("base_ready")
        bias_ps_ready = sem("bias_ps_ready")
        bias_ready = sem("bias_ready")
        rows_made = sem("rows_made")
        h2_ready = sem("h2_ready")
        x2_ready = sem("x2_ready")
        ux_copied = sem("ux_copied")
        STEPS1, STEPS2 = 16, 5
        mask_loaded = [[sem(f"mask_loaded{u}{k}") for k in range(2)] for u in range(2)]
        late_loaded = sem("late_loaded")
        late_made = sem("late_made")
        parts_ready = sem("parts_ready")
        parts_turned = sem("parts_turned")
        own_copied = sem("own_copied")
        far_copied = sem("far_copied")
        norms_ready = sem("norms_ready")
        norms_turned = sem("norms_turned")
        far_n_copied = sem("far_n_copied")
        own_n_copied = sem("own_n_copied")
        row_ready = sem("row_ready")
        row_copied = sem("row_copied")
        xrow_ready = sem("xrow_ready")
        wrapped = sem("wrapped")
        dist_ready = sem("dist_ready")
        apart = sem("apart")
        prod_ready = sem("prod_ready")
        inv_ready = sem("inv_ready")
        nrm_ready = sem("nrm_ready")
        logs_ready = sem("logs_ready")
        atanh_ready = sem("atanh_ready")
        gain_ready = sem("gain_ready")
        dir_ready = sem("dir_ready")
        turn_ready = sem("turn_ready")
        tr_ready = sem("tr_ready")
        dir_used = sem("dir_used")
        tr_used = sem("tr_used")
        quad_ready = sem("quad_ready")
        quad_turned = sem("quad_turned")
        feat_ready = sem("feat_ready")
        sums_read = sem("sums_read")
        lin_ready = sem("lin_ready")
        lin_read = sem("lin_read")
        x3_ready = sem("x3_ready")
        counts_turned = sem("counts_turned")
        counts_copied = sem("counts_copied")
        nv_ready = sem("nv_ready")
        tanh3_ready = sem("tanh3_ready")
        adj4_loaded = [sem(f"adj4_loaded{k}") for k in range(2)]
        exps_made = [sem(f"exps_made{k}") for k in range(2)]
        exps_read = [sem(f"exps_read{k}") for k in range(2)]
        out_made = sem("out_made")
        out_sent = [sem(f"out_sent{k}") for k in range(2)]
        block = ctx.enter_context(nc.Block())

        class Chain:

            def __init__(self, eng, s):
                self.eng, self.s, self.n, self.base = eng, s, 0, 0

            def __call__(self, ins):
                ins.then_inc(self.s, 1)
                self.n += 1
                self.eng.wait_ge(self.s, self.base + self.n)

            def go(self, ins):
                ins.then_inc(self.s, 1)
                self.n += 1

            def turn(self, start, index, steps):
                self.base, self.n = start + index * steps, 0

        def each_pair(eng, body):
            body(0, 0)
            body(1, 1)
            with eng.Fori(2, NC - 1, 2) as c:
                body(c, 0)
                body(c + 1, 1)
            body(NC - 1, 0)

        UNITS = 4 * NC
        QUADS = [(j, min(4, NB - j)) for j in range(0, NB, 4)]
        NQ = len(QUADS)
        GROUP = [(j, min(4, NB - j)) for j in range(0, NB, 4)]
        GROUPS = ((len(GROUP) + 1) // 2, len(GROUP) // 2)
        W_SHIFT = 128.0 * HORIZON - EDGE

        def each_unit(eng, body):
            for k in range(4):
                body(k, k)
            with eng.Fori(1, NC) as s:
                for k in range(4):
                    body(4 * s + k, k)

        def wide(v, n=D):
            return v.unsqueeze(2).broadcast_to([P, v.shape[1], n])

        def pair(t, c):
            return t[:, bass.ds(2 * c, 2)]

        @block.sync
        def _(sp):
            sp.dma_start(x_all[:, :, :], x).then_inc(x_all_loaded, 16)
            for dst, src in ((w0, (w_self, w_neigh, b0)),):
                sp.dma_start(dst[0:D, 0:D], src[0]).then_inc(weights_loaded, 16)
                sp.dma_start(dst[0:D, D:2 * D], src[1]).then_inc(weights_loaded, 16)
                sp.dma_start(dst[D:NW, 0:D], src[2]).then_inc(weights_loaded, 16)
            sp.dma_start(w1u[0:D, 0:D], bt1).then_inc(weights_loaded, 16)
            sp.dma_start(w1h[:, :], w11[0:D, :]).then_inc(weights_loaded, 16)
            sp.dma_start(t_rows[0:1], w11[D:NW, :]).then_inc(weights_loaded, 16)
            sp.dma_start(t_rows[1:2], b11).then_inc(weights_loaded, 16)
            sp.dma_start(t_one[:, :], t1).then_inc(weights_loaded, 16)
            sp.dma_start(w1o[:, :], w12).then_inc(weights_loaded, 16)
            sp.dma_start(w1u[D:NW, D:2 * D], b12).then_inc(weights_loaded, 16)

            def load_x(c, q):
                if not isinstance(c, int) or c >= 2:
                    sp.wait_ge(base_ready, c - 1)
                sp.dma_start(x_in[:, q], pair(x, c)).then_inc(x_in_sem[q], 16)

            load_x(0, 0)
            load_x(1, 1)
            with sp.Fori(2, NC - 1, 2) as c:
                load_x(c, 0)
                load_x(c + 1, 1)
            load_x(NC - 1, 0)

            sp.wait_ge(h2_ready, NC)
            sp.dma_start(w2h[:, :], w_hyp).then_inc(late_loaded, 16)
            sp.dma_start(b2_all[:, :], b_hyp.broadcast_to([P, D])).then_inc(late_loaded, 16)
            sp.dma_start(w3d[:, :], w_dec).then_inc(late_loaded, 16)
            sp.dma_start(b3_all[:, :], b_dec.broadcast_to([P, D])).then_inc(late_loaded, 16)

            def load_mask(i, r, u, s):
                if not isinstance(s, int) or s >= 1:
                    sp.wait_ge(tr_ready, 2 * (4 * s + 2 * r + u) - 6)
                at = u * (UW[0] + 6 * P)
                sp.dma_start(mask[u][r][:, :], adj_mask[i, :, at:at + UW[u] + 6 * P]) \
                    .then_inc(mask_loaded[u][r], 16)

            for r in range(2):
                for u in range(2):
                    load_mask(r, r, u, 0)
            with sp.Fori(1, NC) as s:
                for r in range(2):
                    for u in range(2):
                        load_mask(2 * s + r, r, u, s)

            def send(c, q):
                sp.wait_ge(out_made, c + 1)
                sp.dma_start(pair(out, c), o_buf[:, q]).then_inc(out_sent[q], 16)

            each_pair(sp, send)
            sp.wait_ge(out_sent[0], (NC + 1) // 2 * 16)
            sp.wait_ge(out_sent[1], NC // 2 * 16)

        @block.gpsimd
        def _(pool):
            def load_adj(c, q):
                pool.dma_start(adj[:, c], adj_cols[c]).then_inc(adj_loaded[q], 16)

            load_adj(0, 0)
            load_adj(1, 1)
            step = Chain(pool, pool_step)
            step(pool.memset(ident[:, :], 0.0))
            step(pool.affine_select(out=ident[:, :], in_=ident[:, :], compare_op=ALU.not_equal, fill=1.0,
                                    base=0, pattern=[[-1, P]], channel_multiplier=1))
            pool.memset(ones_row[:, :], 1.0).then_inc(consts_made, 1)
            hot = z_spl[:, :, SPL:SPL + NB]
            step(pool.memset(hot, 0.0))
            pool.affine_select(out=hot, in_=hot, compare_op=ALU.not_equal, fill=1.0,
                                    base=0, pattern=[[1, NB], [-1, NB]], channel_multiplier=0).then_inc(consts_made, 1)

            def next_adj(c, q):
                pool.wait_ge(adj_loaded[q], (c // 2) * 16)
                load_adj(c, q)

            with pool.Fori(2, NC - 3, 2) as c:
                next_adj(c, 0)
                next_adj(c + 1, 1)
            next_adj(NC - 3, 0)
            pool.wait_ge(z_split, NC)
            next_adj(NC - 2, 1)
            next_adj(NC - 1, 0)

            def residual(c, q):
                pool.wait_ge(ux_copied, c + 1)
                xb, u, parts, x2 = ux_in[:, :, 0:D], ux_in[:, :, D:2 * D], pair(xb_spl, c), pair(base, c)
                step.go(pool.tensor_copy(parts[:, :, 0:D], xb))
                step(pool.tensor_tensor(x2, xb, wide(deg[:, bass.ds(2 * c, 2)]), ALU.mult))
                step.go(pool.tensor_tensor(xb, xb, parts[:, :, 0:D], ALU.subtract))
                step(pool.tensor_tensor(x2, x_in[:, q], x2, ALU.subtract))
                step(pool.tensor_copy(parts[:, :, D:2 * D], xb))
                step(pool.tensor_tensor(parts[:, :, 2 * D:SPL], xb, parts[:, :, D:2 * D], ALU.subtract))
                pool.tensor_tensor(x2, x2, u, ALU.add).then_inc(base_ready, 1)

            for c in range(NC):
                residual(c, c % 2)

            def split_rows(c):
                pool.wait_ge(h2_ready, c + 1)
                v, rest, got = pair(h2, c), rows[:, :, 0:D], pair(parts, c)
                part = [got[:, :, k * D:(k + 1) * D] for k in range(TURNS)]
                step(pool.tensor_copy(part[5], v))
                step.go(pool.tensor_tensor(rest, v, part[5], ALU.subtract))
                step.go(pool.tensor_copy(part[2], part[5]))
                step(pool.tensor_copy(part[3], part[5]))
                step(pool.tensor_copy(part[6], rest))
                step.go(pool.tensor_copy(part[0], part[6]))
                step.go(pool.tensor_copy(part[1], part[6]))
                pool.tensor_tensor(part[4], rest, part[6], ALU.subtract).then_inc(parts_ready, 1)
                pool.wait_ge(parts_ready, c + 1)

            pool.wait_ge(agg_ready, NC + 2)
            for c in range(NC):
                split_rows(c)
            pool.wait_ge(h2_ready, NC)
            step(pool.memset(ident16[:, :], 0.0))
            pool.affine_select(out=ident16[:, :], in_=ident16[:, :], compare_op=ALU.not_equal, fill=1.0,
                               base=0, pattern=[[-1, P]], channel_multiplier=1).then_inc(late_made, 1)
            step(pool.memset(order[:, :], 0.0))
            step(pool.affine_select(out=order[:, :], in_=order[:, :], compare_op=ALU.is_ge, fill=-128.0,
                                    base=0, pattern=[[1, P]], channel_multiplier=-1))
            pool.affine_select(out=order[:, :], in_=order[:, :], compare_op=ALU.not_equal, fill=EDGE,
                               base=0, pattern=[[-1, P]], channel_multiplier=1).then_inc(late_made, 1)
            step(pool.memset(pick_b[:, :], 0.0))
            step(pool.affine_select(out=pick_b[:, :], in_=pick_b[:, :], compare_op=ALU.is_ge, fill=-1.0,
                                    base=-3, pattern=[[0, P]], channel_multiplier=1))
            pool.affine_select(out=pick_b[:, :], in_=pick_b[:, :], compare_op=ALU.not_equal, fill=1.0,
                               base=-3, pattern=[[0, P]], channel_multiplier=1).then_inc(late_made, 1)
            pool.tensor_copy(xrow[:, 0:NB, 0:D], h2[:, :, :]).then_inc(xrow_ready, 1)
            pool.tensor_copy(xrow[:, NB:EXB, 0:D], h2[:, 0:EXB - NB, :]).then_inc(xrow_ready, 1)

            def product(t, k):
                pool.wait_ge(apart, t + 1)
                if not isinstance(t, int) or t >= 4:
                    pool.wait_ge(gain_ready, t - 3)
                pool.tensor_tensor(inv[k][:, :], den[:, 0:UW[k % 2]], dist[k % 2][:, :], ALU.mult) \
                    .then_inc(prod_ready, 1)

            def norm(t, k):
                if not isinstance(t, int) or t >= 2:
                    pool.wait_ge(atanh_ready, t - 1)
                pool.wait_ge(inv_ready, t + 1)
                pool.tensor_tensor(nrm[k % 2][:, :], dist[k % 2][:, :], inv[k][:, :], ALU.mult).then_inc(nrm_ready, 1)

            def twice_atanh(t, k):
                u = k % 2
                pool.wait_ge(logs_ready, t + 1)
                pool.tensor_tensor(gain[u][:, :], gain[u][:, :], nrm[u][:, :], ALU.subtract) \
                    .then_inc(atanh_ready, 1)

            def unit(t, k):
                product(t, k)
                if not isinstance(t, int) or t >= 1:
                    norm(t - 1, (k - 1) % 4)
                if not isinstance(t, int) or t >= 2:
                    twice_atanh(t - 2, (k - 2) % 4)

            def load_adj4(c, q):
                pool.dma_start(adj4[q][:, :], adj_cols[c]).then_inc(adj4_loaded[q], 16)

            load_adj4(0, 0)
            each_unit(pool, unit)
            norm(UNITS - 1, 3)
            twice_atanh(UNITS - 2, 2)
            twice_atanh(UNITS - 1, 3)
            pool.wait_ge(tr_used, UNITS)
            load_adj4(1, 1)
            step(pool.memset(later[:, :, :], 0.0))
            pool.affine_select(out=later[:, :, :], in_=later[:, :, :], compare_op=ALU.is_ge, fill=-128.0,
                               base=0, pattern=[[1, NB], [0, P]], channel_multiplier=-1).then_inc(late_made, 1)


            def next_adj4(c, q):
                pool.wait_ge(exps_made[0], GROUPS[0] * (c - 1))
                pool.wait_ge(exps_made[1], GROUPS[1] * (c - 1))
                load_adj4(c, q)

            with pool.Fori(2, NC - 1, 2) as c:
                next_adj4(c, 0)
                next_adj4(c + 1, 1)
            next_adj4(NC - 1, 0)

        @block.scalar
        def _(act):
            step = Chain(act, act_step)

            def settled():
                act.wait_ge(x_all_loaded, 16)

            def root(n, dst, src):
                act.wait_ge(var_ready, n + 1)
                act.activation(dst, src, ACT.Sqrt).then_inc(root_ready, 1)

            def deviation(n, dst, src):
                act.wait_ge(var_ready, n + 1)
                act.activation(dst, src, ACT.Sqrt, scale=1.0 / D, bias=EPS).then_inc(root_ready, 1)

            deviation(0, st_all[:, 2, :], st_all[:, 1, :])
            act.wait_ge(bias_ps_ready, 1)
            act.activation(bias11[:, :], one[:, 0:1], ACT.Copy).then_inc(bias_ready, 1)

            def copy_hT(n):
                act.wait_ge(turned, n + 1)
                act.activation(hT[0:D, :], tp[0:D, 0:CW], ACT.Copy).then_inc(hT_ready, 1)

            def products0(c, q):
                if not isinstance(c, int) or c >= 1:
                    act.wait_ge(z_ready, c)
                copy_hT(c)

            products0(0, 0)
            with act.Fori(1, NC) as c:
                products0(c, 0)

            def layer12(c, q):
                root(2 * c + 1, small[:, 4, :], small[:, 3, :])
                deviation(2 * c + 2, small[:, 9, :], small[:, 8, :])
                copy_hT(NC + c)
                act.wait_ge(hid_ready, c + 1)
                act.activation(hidT[:, :], mm[:, 0:CW], ACT.Tanh, bias=bias11[:, :]).then_inc(tanh_ready, 1)
                act.wait_ge(ux_ready, c + 1)
                if not isinstance(c, int) or c >= 1:
                    act.wait_ge(base_ready, c)
                act.activation(ux_in[:, :, :], ux[:, :, 0:2 * D], ACT.Copy).then_inc(ux_copied, 1)

            each_pair(act, layer12)
            with act.Fori(0, NC) as c:
                deviation(2 * NC + 1 + c, small[:, 9, :], small[:, 8, :])


            act.wait_ge(h2_ready, NC)
            for c in range(NC):
                act.wait_ge(parts_turned, c + 1)
                act.activation(pair(own, c).rearrange("p b k n -> p b (k n)"),
                               agg[:, c % 2 * 2:c % 2 * 2 + 2, 0:3 * P], ACT.Copy, scale=-2.0).then_inc(own_copied, 1)

            def copy_row(k):
                j, n = QUADS[k]
                act.wait_ge(row_ready, k + 1)
                act.activation(x_b_row[:, j * P:(j + n) * P], agg[:, k % 2, 0:n * P], ACT.Copy) \
                    .then_inc(row_copied, 1)

            for k, (j, n) in enumerate(QUADS):
                act.wait_ge(norms_turned, k + 1)
                act.activation(far_n[:, j * P:(j + n) * P], ux_bank[0:KN, 0:n * P], ACT.Copy) \
                    .then_inc(far_n_copied, 1)
                if k >= 1:
                    copy_row(k - 1)
            copy_row(NQ - 1)
            act.preload_act_table_set("natural_log_exp_and_others")

            def inverse(t, k):
                act.wait_ge(prod_ready, t + 1)
                step(act.activation(inv[k][:, :], inv[k][:, :], ACT.Ln, bias=LN_FLOOR))
                act.activation(inv[k][:, :], inv[k][:, :], ACT.Exp, scale=-0.5).then_inc(inv_ready, 1)

            def logs(t, k):
                u = k % 2
                act.wait_ge(nrm_ready, t + 1)
                step(act.activation(nrm[u][:, :], nrm[u][:, :], ACT.Relu, scale=-1.0, bias=TANH_CLIP))
                if not isinstance(t, int) or t >= 2:
                    act.wait_ge(tr_ready, 2 * t - 2)
                    act.wait_ge(dir_ready, t - 1)
                act.activation(gain[u][:, :], nrm[u][:, :], ACT.Ln, scale=-1.0, bias=1.0 + TANH_CLIP)
                act.activation(nrm[u][:, :], nrm[u][:, :], ACT.Ln, bias=1.0 - TANH_CLIP).then_inc(logs_ready, 1)

            def units(s):
                for r in range(2):
                    for u in range(2):
                        k = 2 * r + u
                        t = 4 * s + k
                        step.turn(act3, t, 2)
                        if isinstance(t, int) and t == 0:
                            step.n = 1
                        inverse(t, k)
                        if not isinstance(t, int) or t >= 1:
                            logs(t - 1, (k - 1) % 4)

            act3 = step.n - 1
            units(0)
            with act.Fori(1, NC) as s:
                units(s)
            step.turn(act3, UNITS, 2)
            step.n = 0
            logs(UNITS - 1, 3)

            def copy_feat(i):
                w = QUADS[i % NQ][1] * P
                act.wait_ge(quad_turned, i + 1)
                if i >= 2:
                    act.wait_ge(lin_ready, i - 1)
                act.activation(featT[:, i % 2, 0:w], (tp, ux_bank)[i % 2][0:D, 0:w], ACT.Copy) \
                    .then_inc(feat_ready, 1)

            for k, (j, n) in enumerate(QUADS):
                act.wait_ge(counts_turned, k + 1)
                act.activation(countsT[:, j * P:(j + n) * P], agg[0:NB, k % 2, 0:n * P], ACT.Copy) \
                    .then_inc(counts_copied, 1)
            for i in range(NQ):
                copy_feat(i)
            root(3 * NC + 1, pn[:, 6, :], pn[:, 5, :])
            act.wait_ge(nv_ready, 1)
            act.activation(pn[:, 7, :], pn[:, 6, :], ACT.Tanh).then_inc(tanh3_ready, 1)
            deviation(3 * NC + 2, pn[:, 2, :], pn[:, 3, :])
            for i in range(NQ, 2 * NQ):
                copy_feat(i)

            def weights(c, q):
                for g, (j, n) in enumerate(GROUP):
                    if g % 2 == 0:
                        act.wait_ge(exps_made[0], GROUPS[0] * c + g // 2 + 1)
                        if g == 0 and (not isinstance(c, int) or c >= 2):
                            act.wait_ge(agg_ready, 2 * NC + c - 1)
                        act.activation(w_exp[q][:, j:j + n, :].rearrange("p j n -> p (j n)"),
                                       exp_ps[0][:, 0:n * CW], ACT.Relu, bias=W_SHIFT) \
                            .then_inc(exps_read[0], 1)

            each_pair(act, weights)

        @block.tensor
        def _(pe):
            pe.wait_ge(weights_loaded, 160)
            pe.wait_ge(consts_made, 2)
            pe.wait_ge(rows_made, 4)
            pe.matmul(one[:, 0:1], t_rows, t_one[:, :], start=True, stop=True).then_inc(bias_ps_ready, 1)

            def turn_pair(src, n):
                pe.wait_ge(h_ready, n + 1)
                if not isinstance(n, int) or n >= 1:
                    pe.wait_ge(hT_ready, n)
                pe.matmul(tp[0:D, 0:P], src[:, 0, :], ident[:, :], start=True, stop=True)
                pe.matmul(tp[0:D, P:CW], src[:, 1, :], ident[:, :], start=True, stop=True).then_inc(turned, 1)

            def products0(c, q):
                turn_pair(h_pair[:, q], c)
                pe.wait_ge(hT_ready, c + 1)
                if not isinstance(c, int) or c >= 2:
                    pe.wait_ge(z_split, c - 1)
                for b in range(2):
                    ins = pe.matmul((mm, one)[q][:, b * P:(b + 1) * P], hT[:, b * P:(b + 1) * P], w0[:, :],
                                    start=True, stop=True)
                ins.then_inc(z_ready, 1)

            pe.wait_ge(bias_ready, 1)
            products0(0, 0)
            products0(1, 1)
            with pe.Fori(2, NC - 1, 2) as c:
                products0(c, 0)
                products0(c + 1, 1)
            products0(NC - 1, 0)

            def gather(c, q, n, terms, width):
                if not isinstance(n, int) or n >= 2:
                    pe.wait_ge(agg_read, n - 1)
                for b in range(2):
                    for j in range(NB):
                        ins = pe.matmul(agg[:, 2 * q + b, 0:width],
                                        adj[:, c, j * CW + b * P:j * CW + (b + 1) * P],
                                        terms[:, j, 0:width], start=(j == 0), stop=(j == NB - 1))
                ins.then_inc(agg_ready, 1)

            def products1(c):
                turn_pair(t_c, NC + c)
                pe.wait_ge(hT_ready, NC + c + 1)
                if not isinstance(c, int) or c >= 1:
                    pe.wait_ge(ux_copied, c)
                    pe.wait_ge(tanh_ready, c)
                pe.matmul(mm[:, 0:CW], w1h[:, :], hT[0:D, :], start=True, stop=True).then_inc(hid_ready, 1)
                for b in range(2):
                    pe.matmul(ux[:, b, 0:2 * D], hT[:, b * P:(b + 1) * P], w1u[:, :], start=b == 0, stop=False,
                              skip_group_check=True)
                pe.wait_ge(tanh_ready, c + 1)
                for b in range(2):
                    ins = pe.matmul(ux[:, b, D:2 * D], hidT[:, b * P:(b + 1) * P], w1o[:, :],
                                    start=False, stop=b == 1, skip_group_check=True)
                ins.then_inc(ux_ready, 1)

            def layer1(c, q):
                pe.wait_ge(adj_loaded[q], (c // 2 + 1) * 16)
                gather(c, q, c, z_spl, SPL + NB)
                if not isinstance(c, int) or c >= 1:
                    products1(c - 1)

            pe.wait_ge(z_split, NC)
            for c in range(NC):
                layer1(c, c % 2)
            products1(NC - 1)
            pe.wait_ge(base_ready, NC)

            for c in range(NC):
                gather(c, 1 - c % 2, NC + c, xb_spl, SPL)


            pe.wait_ge(late_made, 1)
            pe.wait_ge(agg_read, 2 * NC)
            for c in range(NC):
                pe.wait_ge(parts_ready, c + 1)
                if c >= 2:
                    pe.wait_ge(own_copied, c - 1)
                    pe.wait_ge(far_copied, c - 1)
                for b in range(2):
                    i = 2 * c + b
                    for k, first in enumerate((0, 2, 3)):
                        pe.matmul(agg[:, c % 2 * 2 + b, k * P:(k + 1) * P],
                                  parts[:, i, first * D:first * D + P], ident16[:, :], start=True, stop=True)
                    for k, first in enumerate((5, 4)):
                        ins = pe.matmul(side_ps[c % 2][:, b, k, :], parts[:, i, first * D:first * D + P],
                                        ident16[:, :], start=True, stop=True)
                ins.then_inc(parts_turned, 1)

            def row(k):
                j, n = QUADS[k]
                pe.wait_ge(far_n_copied, k + 1)
                if k >= 2:
                    pe.wait_ge(row_copied, k - 1)
                pe.matmul(agg[:, k % 2, 0:n * P], pick_b[:, :], far_n[:, j * P:(j + n) * P],
                          start=True, stop=True).then_inc(row_ready, 1)

            pe.wait_ge(norms_ready, 1)
            pe.wait_ge(own_copied, NC)
            pe.wait_ge(late_made, 3)
            for k, (j, n) in enumerate(QUADS):
                if k >= 1:
                    pe.wait_ge(far_n_copied, k)
                    pe.wait_ge(own_n_copied, k)
                for first, bank in ((0, ux_bank), (3, one)):
                    for m in range(n):
                        ins = pe.matmul(bank[0:KN, m * P:(m + 1) * P], norms[:, j + m, first:first + KN],
                                        ident16[:, :], start=True, stop=True)
                ins.then_inc(norms_turned, 1)
                if k >= 1:
                    row(k - 1)
            row(NQ - 1)
            pe.wait_ge(row_copied, NQ)
            pe.wait_ge(wrapped, 5)
            for b in range(4):
                pe.matmul(agg[:, b, :], ones_row[:, :], zero_row[:, :], start=True, stop=False,
                          skip_group_check=True)

            def distances(s, r, u):
                t = 4 * s + 2 * r + u
                if t >= 1:
                    pe.wait_ge(apart, t)
                i = 2 * s + r
                for k, (w, v) in enumerate(((own[:, i, 0, :], far12), (own[:, i, 1, :], far12),
                                            (own[:, i, 2, :], far31), (own_n[:, i * P:(i + 1) * P], far_n))):
                    for at in range(0, UW[u], 512):
                        n = min(512, UW[u] - at)
                        col = s * CW + UO[u] * P + at
                        ins = pe.matmul(dist_ps[:, at:at + n], w, v[:, col:col + n], start=k == 0, stop=k == 3)
                ins.then_inc(dist_ready, 1)

            def sums(s, r, u):
                t = 4 * s + 2 * r + u
                pe.wait_ge(gain_ready, t + 1)
                for h in range(2):
                    if not isinstance(t, int) or t >= 1:
                        pe.wait_ge(tr_ready, 2 * t - 1 + h)
                    for k in range(3):
                        at = (UT[u] - UO[u] + 3 * h + k) * P
                        ins = pe.transpose(turn_ps[:, h, k * P:(k + 1) * P], gain[u][:, at:at + P], ident[:, :])
                    ins.then_inc(turn_ready, 1)
                pe.wait_ge(dir_ready, t + 1)
                for k in range(UB[u]):
                    j = (2 * s + UO[u] + k) % NB
                    ins = pe.matmul(lo[:, bass.ds(acc_at(j), NW)], p_dir[u][:, k * P:(k + 1) * P],
                                    xrow[:, 2 * s + r, :], start=False, stop=False, skip_group_check=True)
                ins.then_inc(dir_used, 1)
                for h in range(2):
                    pe.wait_ge(tr_ready, 2 * t + 1 + h)
                    for k in range(3):
                        m = 3 * h + k
                        ins = pe.matmul(lo[:, bass.ds(acc_at(2 * s + r), NW)], p_tr[u][:, m * P:(m + 1) * P],
                                        xrow[:, 2 * s + UT[u] + m, :], start=False, stop=False,
                                        skip_group_check=True)
                ins.then_inc(tr_used, 1)

            def units(s):
                for r in range(2):
                    for u in range(2):
                        last = isinstance(s, int) and s == NC - 1 and r == 1 and u == 1
                        k = 2 * r + u
                        if not last:
                            distances(s + (k + 1) // 4, (k + 1) // 2 % 2, (k + 1) % 2)
                        if k == 3:
                            sums(s, 0, 0)
                        elif not isinstance(s, int) or s >= 1:
                            sums(s - 1, (k + 1) // 2, (k + 1) % 2)

            distances(0, 0, 0)
            for s in range(NC):
                units(s)
            sums(NC - 1, 0, 1)
            sums(NC - 1, 1, 0)
            sums(NC - 1, 1, 1)
            pe.wait_ge(late_loaded, 64)

            pe.wait_ge(sums_read, 1)
            for k, (j, n) in enumerate(QUADS):
                if k >= 2:
                    pe.wait_ge(counts_copied, k - 1)
                for m in range(n):
                    ins = pe.matmul(agg[0:NB, k % 2, m * P:(m + 1) * P], counts[:, j + m, :],
                                    ident16[:, :], start=True, stop=True)
                ins.then_inc(counts_turned, 1)

            def turn_quad(i):
                pe.wait_ge(quad_ready, i + 1)
                if i >= 2:
                    pe.wait_ge(feat_ready, i - 1)
                for m in range(QUADS[i % NQ][1]):
                    ins = pe.transpose((tp, ux_bank)[i % 2][0:D, m * P:(m + 1) * P], row_quad[:, i % 2, m, :],
                                       ident[:, :])
                ins.then_inc(quad_turned, 1)

            def linear(i, w):
                pe.wait_ge(feat_ready, i + 1)
                if i >= 2:
                    pe.wait_ge(lin_read, i - 1)
                for m in range(QUADS[i % NQ][1]):
                    ins = pe.matmul((mm, one)[i % 2][:, m * D:(m + 1) * D], featT[:, i % 2, m * P:(m + 1) * P],
                                    w[:, :], start=True, stop=True)
                ins.then_inc(lin_ready, 1)

            for first, w in ((0, w2h), (NQ, w3d)):
                turn_quad(first)
                for i in range(first, first + NQ):
                    if i + 1 < first + NQ:
                        turn_quad(i + 1)
                    linear(i, w)
            pe.wait_ge(lin_read, 2 * NQ)
            pe.wait_ge(counts_copied, NQ)
            pe.wait_ge(late_made, 4)

            def exponents(c, q):
                pe.wait_ge(adj4_loaded[q], (c // 2 + 1) * 16)
                for g, (j, n) in enumerate(GROUP):
                    k = g % 2
                    if g >= 2 or not isinstance(c, int) or c >= 1:
                        pe.wait_ge(exps_read[k], GROUPS[k] * c + g // 2)
                    for m in range(n):
                        dst = exp_ps[k][:, m * CW:(m + 1) * CW]
                        pe.matmul(dst, order[:, :], adj4[q][:, (j + m) * CW:(j + m + 1) * CW],
                                  start=True, stop=False)
                        ins = pe.matmul(dst, later[:, j + m, :], countsT[:, bass.ds(c * CW, CW)],
                                        start=False, stop=True)
                    ins.then_inc(exps_made[k], 1)

            def decayed(c, q):
                for k in range(2):
                    pe.wait_ge(exps_read[k], GROUPS[k] * (c + 1))
                if not isinstance(c, int) or c >= 2:
                    pe.wait_ge(agg_read, 2 * NC + c - 1)
                for b in range(2):
                    for j in range(NB):
                        ins = pe.matmul(agg[:, 2 * q + b, 0:SPL],
                                        w_exp[q][:, j, b * P:(b + 1) * P].bitcast(bf16),
                                        s_spl[:, j, :], start=(j == 0), stop=(j == NB - 1))
                ins.then_inc(agg_ready, 1)

            def layer4(c, q):
                exponents(c, q)
                if not isinstance(c, int) or c >= 1:
                    decayed(c - 1, 1 - q)

            for c in range(NC):
                layer4(c, c % 2)
            decayed(NC - 1, 0)

        @block.vector
        def _(dve):
            step = Chain(dve, dve_step)
            s = [small[:, k, :] for k in range(16)]

            def root(n):
                dve.wait_ge(root_ready, n + 1)

            dve.memset(hT[D:NW, :], 1.0).then_inc(rows_made, 1)
            dve.memset(w0[D:NW, D:2 * D], 0.0).then_inc(rows_made, 1)
            dve.memset(w1u[0:D, D:2 * D], 0.0).then_inc(rows_made, 1)
            dve.memset(w1u[D:NW, 0:D], 0.0).then_inc(rows_made, 1)
            dve.wait_ge(x_all_loaded, 16)
            sa = [st_all[:, k, :] for k in range(4)]
            step(dve.tensor_reduce(sa[0], x_all[:, :, :], AX, ALU.add))
            step(dve.scalar_tensor_tensor(x_all[:, :, :], wide(sa[0]), -1.0 / D, x_all[:, :, :], ALU.mult, ALU.add))
            step(dve.tensor_tensor(sq_all[:, :, :], x_all[:, :, :], x_all[:, :, :], ALU.mult))
            dve.tensor_reduce(sa[1], sq_all[:, :, :], AX, ALU.add).then_inc(var_ready, 1)
            root(0)
            step(dve.reciprocal(sa[3], sa[2]))

            def norm0(c, q):
                if not isinstance(c, int) or c >= 2:
                    dve.wait_ge(turned, c - 1)
                dve.scalar_tensor_tensor(h_pair[:, q], pair(x_all, c), 0.0, wide(sa[3][:, bass.ds(2 * c, 2)]),
                                         ALU.max, ALU.mult).then_inc(h_ready, 1)

            def split(chain, dst, v, rest, last):
                chain(dve.tensor_copy(dst[:, :, 0:D], v))
                chain(dve.tensor_tensor(rest, v, dst[:, :, 0:D], ALU.subtract))
                chain(dve.tensor_copy(dst[:, :, D:2 * D], rest))
                dve.tensor_tensor(dst[:, :, 2 * D:SPL], rest, dst[:, :, D:2 * D], ALU.subtract).then_inc(last, 1)

            def split0(c, q):
                step.turn(start, c, 4)
                dve.wait_ge(z_ready, c + 1)
                m = (mm, one)[q][:, 0:CW].rearrange("p (b n) -> p b n", b=2)
                step(dve.tensor_copy(pair(base, c), m[:, :, 0:D]))
                split(step, pair(z_spl, c), m[:, :, D:2 * D], t_b[:, :, :], z_split)

            start = step.n
            norm0(0, 0)
            norm0(1, 1)
            with dve.Fori(0, NC - 3, 2) as c:
                split0(c, 0)
                norm0(c + 2, 0)
                split0(c + 1, 1)
                norm0(c + 3, 1)
            split0(NC - 3, 0)
            norm0(NC - 1, 0)
            split0(NC - 2, 1)
            split0(NC - 1, 0)

            def layer_norm(v, h, n, event):
                step(dve.tensor_reduce(s[7], v, AX, ALU.add))
                step(dve.scalar_tensor_tensor(t_b[:, :, :], wide(s[7]), -1.0 / D, v, ALU.mult, ALU.add))
                step(dve.tensor_tensor(t_c[:, :, :], t_b[:, :, :], t_b[:, :, :], ALU.mult))
                dve.tensor_reduce(s[8], t_c[:, :, :], AX, ALU.add).then_inc(var_ready, 1)
                root(n)
                step(dve.reciprocal(s[10], s[9]))
                dve.scalar_tensor_tensor(h, t_b[:, :, :], 0.0, wide(s[10]), ALU.max, ALU.mult) \
                    .then_inc(event, 1)

            def sum_parts(v):
                return v.rearrange("p b (k d) -> p b d k", k=3)

            def layer12(c, q):
                step.turn(start1, c, STEPS1)
                dve.wait_ge(agg_ready, c + 1)
                got = agg[:, 2 * q:2 * q + 2, :]
                step.go(dve.tensor_tensor(rows[:, :, :], got[:, :, 0:SPL], pair(z_spl, c)[:, :, 0:SPL], ALU.add))
                step.go(dve.tensor_copy(pair(counts, c), got[:, :, SPL:SPL + NB]))
                dve.tensor_reduce(deg[:, bass.ds(2 * c, 2)], got[:, :, SPL:SPL + NB], AX, ALU.add) \
                    .then_inc(agg_read, 1)
                dve.wait_ge(agg_read, c + 1)
                step.go(dve.tensor_scalar(s[1], deg[:, bass.ds(2 * c, 2)], 1.0, 1.0, ALU.add, ALU.max))
                step(dve.tensor_reduce(t_a[:, :, :], sum_parts(rows[:, :, :]), AX, ALU.add))
                step(dve.reciprocal(s[2], s[1]))
                step(dve.tensor_tensor(t_a[:, :, :], t_a[:, :, :], wide(s[2]), ALU.mult))
                step(dve.tensor_tensor(t_a[:, :, :], t_a[:, :, :], pair(base, c), ALU.add))
                step(dve.scalar_tensor_tensor(t_b[:, :, :], t_a[:, :, :], 0.0, t_a[:, :, :], ALU.max, ALU.mult))
                dve.tensor_reduce(s[3], t_b[:, :, :], AX, ALU.add).then_inc(var_ready, 1)
                root(2 * c + 1)
                step(dve.tensor_scalar(s[5], s[4], L2_EPS, None, ALU.max))
                step(dve.reciprocal(s[6], s[5]))
                step(dve.scalar_tensor_tensor(t_b[:, :, :], t_a[:, :, :], 0.0, wide(s[6]), ALU.max, ALU.mult))
                dve.wait_ge(x_in_sem[q], (c // 2 + 1) * 16)
                step(dve.tensor_tensor(x_in[:, q], t_b[:, :, :], x_in[:, q], ALU.add))
                if not isinstance(c, int) or c >= 1:
                    dve.wait_ge(turned, NC + c)
                layer_norm(x_in[:, q], t_c[:, :, :], 2 * c + 2, h_ready)
                assert step.n == STEPS1, step.n

            start1 = start + 4 * NC
            each_pair(dve, layer12)

            def layer2(c, q):
                step.turn(start2, c, STEPS2)
                dve.wait_ge(agg_ready, NC + c + 1)
                dve.tensor_reduce(t_a[:, :, :], sum_parts(agg[:, 2 * q:2 * q + 2, 0:SPL]), AX, ALU.add) \
                    .then_inc(agg_read, 1)
                dve.wait_ge(agg_read, NC + c + 1)
                step(dve.tensor_tensor(t_a[:, :, :], t_a[:, :, :], pair(base, c), ALU.add))
                dve.tensor_scalar(pair(base, c), t_a[:, :, :], 0.0, None, ALU.add).then_inc(x2_ready, 1)
                layer_norm(t_a[:, :, :], pair(h2, c), 2 * NC + 1 + c, h2_ready)
                assert step.n == STEPS2, step.n

            start2 = start1 + STEPS1 * NC
            with dve.Fori(0, NC - 1, 2) as c:
                layer2(c, 1)
                layer2(c + 1, 0)
            layer2(NC - 1, 1)

            start3 = start2 + STEPS2 * NC
            step.turn(start3, 0, 0)
            dve.wait_ge(h2_ready, NC)
            sq = squares[:, :, :]
            step(dve.tensor_tensor(sq, h2[:, :, :], h2[:, :, :], ALU.mult))
            step(dve.tensor_reduce(x2[:, :], sq, AX, ALU.add))
            step(dve.memset(zero_row[:, :], 0.0))
            step(dve.memset(norms[:, :, 3:6], 1.0))
            n2 = x2[:, :].unsqueeze(2)
            rest, rest3 = pn[:, 0, :], pn[:, 0, :].unsqueeze(2)
            step(dve.tensor_copy(norms[:, :, 0:1], n2))
            step.go(dve.tensor_copy(norms[:, :, 6:7], n2))
            step(dve.tensor_tensor(rest3, n2, norms[:, :, 0:1], ALU.subtract))
            step.go(dve.tensor_copy(norms[:, :, 1:2], rest3))
            step(dve.tensor_copy(norms[:, :, 7:8], rest3))
            step(dve.tensor_tensor(norms[:, :, 2:3], rest3, norms[:, :, 1:2], ALU.subtract))
            dve.tensor_copy(norms[:, :, 8:9], norms[:, :, 2:3]).then_inc(norms_ready, 1)
            for c in range(NC):
                dve.wait_ge(parts_turned, c + 1)
                got = side_ps[c % 2]
                for k, far in ((0, far12), (1, far31)):
                    ins = dve.tensor_copy(far[:, c * CW:(c + 1) * CW].rearrange("p (b n) -> p b n", b=2),
                                          got[:, :, k, :])
                    step.go(ins) if k == 0 else ins.then_inc(far_copied, 1)
            step(dve.tensor_scalar(x_b[:, :], x2[:, :], -1.0, 1.0, ALU.mult, ALU.add))
            for k, (j, n) in enumerate(QUADS):
                dve.wait_ge(norms_turned, k + 1)
                dve.tensor_copy(own_n[:, j * P:(j + n) * P], one[0:KN, 0:n * P]).then_inc(own_n_copied, 1)
            dve.wait_ge(far_copied, NC)
            for far in (far12, far31):
                dve.tensor_copy(far[:, NP:EXB * P], far[:, 0:EXB * P - NP]).then_inc(wrapped, 1)
            dve.wait_ge(xrow_ready, 2)
            step.go(dve.tensor_scalar(xrow[:, 0:NB, D:NW], n2, 1.0, None, ALU.add))
            dve.tensor_scalar(xrow[:, NB:EXB, D:NW], x2[:, 0:EXB - NB].unsqueeze(2), 1.0, None, ALU.add) \
                .then_inc(wrapped, 1)
            dve.wait_ge(far_n_copied, NQ)
            dve.tensor_copy(far_n[:, NP:EXB * P], far_n[:, 0:EXB * P - NP]).then_inc(wrapped, 1)
            dve.wait_ge(row_copied, NQ)
            dve.tensor_copy(x_b_row[:, NP:EXB * P], x_b_row[:, 0:EXB * P - NP]).then_inc(wrapped, 1)
            dve.wait_ge(wrapped, 5)
            start3 += step.n
            step.turn(start3, 0, 0)

            def front(s, r, u):
                t = 4 * s + 2 * r + u
                if not isinstance(t, int) or t >= 1:
                    dve.wait_ge(prod_ready, t)
                dve.wait_ge(dist_ready, t + 1)
                d, w = den[:, 0:UW[u]], dist_ps[:, 0:UW[u]]
                step(dve.scalar_tensor_tensor(d, x_b_row[:, bass.ds(s * CW + UO[u] * P, UW[u])],
                                              x_b[:, bass.ds(2 * s + r, 1)], w, ALU.mult, ALU.add))
                step(dve.tensor_scalar(d, d, MIN_NORM, None, ALU.max))
                if not isinstance(t, int) or t >= 2:
                    dve.wait_ge(nrm_ready, t - 1)
                dve.scalar_tensor_tensor(dist[u][:, :], d, NORM_FLOOR, w, ALU.mult, ALU.max) \
                    .then_inc(apart, 1)

            def back(s, r, u):
                t = 4 * s + 2 * r + u
                dve.wait_ge(atanh_ready, t + 1)
                dve.scalar_tensor_tensor(gain[u][:, :], gain[u][:, :], 0.5, inv[2 * r + u][:, :], ALU.mult, ALU.mult) \
                    .then_inc(gain_ready, 1)
                dve.wait_ge(gain_ready, t + 1)
                dve.wait_ge(mask_loaded[u][r], 16 * s + 16)
                if not isinstance(t, int) or t >= 2:
                    dve.wait_ge(dir_used, t - 1)
                dve.tensor_tensor(p_dir[u][:, :], gain[u][:, :], mask[u][r][:, 0:UW[u]], ALU.mult) \
                    .then_inc(dir_ready, 1)
                if not isinstance(t, int) or t >= 2:
                    dve.wait_ge(tr_used, t - 1)
                for h in range(2):
                    dve.wait_ge(turn_ready, 2 * t + h + 1)
                    dve.tensor_tensor(p_tr[u][:, 3 * h * P:3 * (h + 1) * P], turn_ps[:, h, 0:3 * P],
                                      mask[u][r][:, UW[u] + 3 * h * P:UW[u] + 3 * (h + 1) * P], ALU.mult) \
                        .then_inc(tr_ready, 1)

            def units(s):
                for k in range(4):
                    step.turn(start3, 4 * s + k, 2)
                    front(s, k // 2, k % 2)
                    if k == 3:
                        back(s, 0, 0)
                    elif not isinstance(s, int) or s >= 1:
                        back(s - 1, (k + 1) // 2, (k + 1) % 2)

            start3 += step.n
            units(0)
            with dve.Fori(1, NC) as s:
                units(s)
            start3 += 2 * UNITS
            step.turn(start3, 0, 0)
            back(NC - 1, 0, 1)
            back(NC - 1, 1, 0)
            back(NC - 1, 1, 1)

            dve.wait_ge(tr_used, UNITS)
            u_sum, tmp, lin = post[0], post[1], post[2]
            p = [pn[:, k, :] for k in range(8)]
            for b in range(4):
                at, n = 7 * b, min(7, NB - 7 * b)
                got = agg[:, b, 0:504].rearrange("p (k n) -> p k n", k=7)[:, 0:n]
                step.go(dve.tensor_tensor(tmp[:, at:at + n, :], got[:, :, 0:D], h2[:, at:at + n, :], ALU.mult))
                step.go(dve.tensor_tensor(u_sum[:, at:at + n, :], got[:, :, 0:D], wide(x_b[:, at:at + n]), ALU.mult))
                ins = dve.tensor_copy(pn[:, 0, at:at + n].unsqueeze(2), got[:, :, D:NW])
                step(ins) if b < 3 else ins.then_inc(sums_read, 1)
            dve.wait_ge(sums_read, 1)
            step(dve.tensor_reduce(p[1], tmp[:, :, :], AX, ALU.add))
            step(dve.scalar_tensor_tensor(p[2], p[1], -2.0, p[0], ALU.mult, ALU.add))
            step(dve.tensor_tensor(tmp[:, :, :], h2[:, :, :], wide(p[2]), ALU.mult))
            step(dve.tensor_tensor(u_sum[:, :, :], u_sum[:, :, :], tmp[:, :, :], ALU.subtract))
            step(dve.tensor_scalar(p[3], deg[:, :], 1e-8, None, ALU.max))
            step(dve.reciprocal(p[4], p[3]))
            step(dve.tensor_scalar(p[3], x_b[:, :], MIN_NORM, None, ALU.max))
            step(dve.tensor_tensor(p[3], p[3], p[4], ALU.mult))

            def rows_out(i, v, scale, op0):
                j, n = QUADS[i % NQ]
                if i >= 2:
                    dve.wait_ge(quad_turned, i - 1)
                dve.scalar_tensor_tensor(row_quad[:, i % 2, 0:n], v[:, j:j + n], 0.0 if op0 == ALU.max else 1.0,
                                         wide(scale[:, j:j + n]), op0, ALU.mult).then_inc(quad_ready, 1)

            def product(i):
                dve.wait_ge(lin_ready, i + 1)
                n = QUADS[i % NQ][1]
                return (mm, one)[i % 2][:, 0:n * D].rearrange("p (b n) -> p b n", b=n)

            def take(i):
                j, n = QUADS[i]
                dve.tensor_tensor(lin[:, j:j + n], product(i), b2_all[:, :].unsqueeze(1).broadcast_to([P, n, D]),
                                  ALU.add).then_inc(lin_read, 1)

            def ahead(first, out_of, into):
                out_of(first)
                out_of(first + 1)
                for i in range(first, first + NQ):
                    into(i)
                    if i + 2 < first + NQ:
                        out_of(i + 2)

            dve.wait_ge(late_loaded, 64)
            ahead(0, lambda i: rows_out(i, u_sum, p[3], ALU.mult), take)
            dve.wait_ge(lin_read, NQ)
            step(dve.tensor_tensor(tmp[:, :, :], lin[:, :, :], lin[:, :, :], ALU.mult))
            dve.tensor_reduce(p[5], tmp[:, :, :], AX, ALU.add).then_inc(var_ready, 1)
            root(3 * NC + 1)
            dve.tensor_scalar(p[6], p[6], MIN_NORM, None, ALU.max).then_inc(nv_ready, 1)
            dve.wait_ge(nv_ready, 1)
            step(dve.reciprocal(p[5], p[6]))
            dve.wait_ge(tanh3_ready, 1)
            step(dve.tensor_tensor(p[7], p[7], p[5], ALU.mult))
            step(dve.tensor_tensor(lin[:, :, :], lin[:, :, :], wide(p[7]), ALU.mult))
            dve.tensor_tensor(base[:, :, :], base[:, :, :], lin[:, :, :], ALU.add).then_inc(x3_ready, 1)
            dve.wait_ge(x3_ready, 1)

            hc, sq4 = post[0], post[1]
            step(dve.tensor_reduce(p[0], base[:, :, :], AX, ALU.add))
            step(dve.scalar_tensor_tensor(hc[:, :, :], wide(p[0]), -1.0 / D, base[:, :, :], ALU.mult, ALU.add))
            step(dve.tensor_tensor(sq4[:, :, :], hc[:, :, :], hc[:, :, :], ALU.mult))
            dve.tensor_reduce(p[3], sq4[:, :, :], AX, ALU.add).then_inc(var_ready, 1)
            step(dve.tensor_tensor(base[:, :, :], base[:, :, :],
                                   b3_all[:, :].unsqueeze(1).broadcast_to([P, NB, D]), ALU.add))
            root(3 * NC + 2)
            step(dve.reciprocal(p[3], p[2]))

            def split4(i):
                j, n = QUADS[i % NQ]
                split(step, s_spl[:, j:j + n], product(i), t_quad[:, 0:n], lin_read)

            ahead(NQ, lambda i: rows_out(i, hc, p[3], ALU.max), split4)
            start4 = start3 + step.n

            def layer4(c, q):
                for g, (j, n) in enumerate(GROUP):
                    if g % 2 == 1:
                        dve.wait_ge(exps_made[1], GROUPS[1] * c + g // 2 + 1)
                        if g == 1 and (not isinstance(c, int) or c >= 2):
                            dve.wait_ge(agg_ready, 2 * NC + c - 1)
                        dve.tensor_scalar(w_exp[q][:, j:j + n, :].rearrange("p j n -> p (j n)"),
                                          exp_ps[1][:, 0:n * CW], W_SHIFT, 0.0, ALU.add, ALU.max) \
                            .then_inc(exps_read[1], 1)

            def result(c, q):
                step.turn(start4, c, 1)
                dve.wait_ge(agg_ready, 2 * NC + c + 1)
                dve.tensor_reduce(t_a[:, :, :], sum_parts(agg[:, 2 * q:2 * q + 2, 0:SPL]), AX, ALU.add) \
                    .then_inc(agg_read, 1)
                dve.wait_ge(agg_read, 2 * NC + c + 1)
                if not isinstance(c, int) or c >= 2:
                    dve.wait_ge(out_sent[q], c // 2 * 16)
                step(dve.tensor_scalar(t_a[:, :, :], t_a[:, :, :], 2.0 ** (127 - HORIZON), None, ALU.mult))
                dve.tensor_tensor(o_buf[:, q], t_a[:, :, :], pair(base, c), ALU.add).then_inc(out_made, 1)
                dve.wait_ge(out_made, c + 1)

            def both(c, q):
                layer4(c, q)
                if not isinstance(c, int) or c >= 2:
                    result(c - 2, q)

            dve.wait_ge(lin_read, 2 * NQ)
            each_pair(dve, both)
            result(NC - 2, 1)
            result(NC - 1, 0)


def kernel(x, adj, L0_gnn_W, L0_gnn_b, L1_gnn_t, L1_gnn_B, L1_gnn_W1, L1_gnn_b1, L1_gnn_W2, L1_gnn_b2,
           L2_gnn_weight, L2_gnn_bias, L3_gnn_weight, L3_gnn_bias):
    import numpy as np
    import concourse.bacc as bacc
    from concourse.bass_utils import run_bass_kernel_spmd

    x, adj = np.asarray(x), np.asarray(adj)
    rows = np.zeros((NP, D), x.dtype)
    rows[:N] = x
    rows = rows.reshape(NB, P, D).transpose(1, 0, 2)
    turned = np.zeros((NP, NP), adj.dtype)
    turned[:N, :N] = adj.T
    cols = turned.reshape(NB, P, NC, CW).transpose(2, 1, 0, 3).reshape(NC, P, NB * CW)
    tiles = turned.reshape(NB, P, NB, P)
    mask = np.empty((NB, P, NB, P), adj.dtype)
    for i in range(NB):
        first = i // 2 * 2
        at = 0
        for u in range(2):
            for k in range(UO[u], UO[u] + UB[u]):
                mask[i, :, at] = tiles[i, :, (first + k) % NB]
                at += 1
            for k in range(UT[u], UT[u] + 6):
                mask[i, :, at] = tiles[(first + k) % NB, :, i]
                at += 1
    w0, w1 = np.asarray(L0_gnn_W), np.asarray(L1_gnn_W1)
    laid = dict(x=rows, adj_cols=cols, adj_mask=mask.reshape(NB, P, NP),
                w_self=w0[:D], w_neigh=w0[D:], b0=np.asarray(L0_gnn_b).reshape(1, D),
                t1=np.stack([np.asarray(L1_gnn_t), np.ones_like(L1_gnn_t)]), bt1=np.asarray(L1_gnn_B).T, w11=w1,
                b11=np.asarray(L1_gnn_b1).reshape(1, HID), w12=np.asarray(L1_gnn_W2),
                b12=np.asarray(L1_gnn_b2).reshape(1, D),
                w_hyp=np.asarray(L2_gnn_weight), b_hyp=np.asarray(L2_gnn_bias).reshape(1, D),
                w_dec=np.asarray(L3_gnn_weight), b_dec=np.asarray(L3_gnn_bias).reshape(1, D))
    nc = bacc.Bacc("TRN2", target_bir_lowering=False, num_devices=1)
    arrays, args = {}, []
    for name, a in laid.items():
        arrays[f"in_{name}"] = np.ascontiguousarray(a)
        args.append(nc.dram_tensor(f"in_{name}", a.shape, mybir.dt.from_np(a.dtype), kind="ExternalInput").ap())
    args.append(nc.dram_tensor("out_rows", (P, NB, D), mybir.dt.float32, kind="ExternalOutput").ap())
    gnn_stack(nc, *args)
    got = run_bass_kernel_spmd(nc, [arrays], core_ids=[0]).results[0]["out_rows"]
    return np.ascontiguousarray(np.asarray(got).transpose(1, 0, 2).reshape(NP, D)[:N])
```

```python
import concourse.bass as bass
from concourse import mybir
from contextlib import ExitStack

N = 3327
D = 64
HID = 128
P = 128
NB = 26
NP = NB * P
NC = NB // 2
CW = 2 * P
TURNS = 7
KN = 6
NW = D + 1
SPL = 3 * D
EXB = 38
UB = (8, 6)
UO = (0, 8)
UT = (2, 8)
HORIZON = 100
EDGE = 16384.0
MIN_NORM = 1e-15
LN_FLOOR = 2.0 ** -63
TANH_CLIP = 1.0 - 168 * 2.0 ** -24
EPS = 1e-05
L2_EPS = 1e-12
NORM_FLOOR = 2.0 ** -22


def gnn_stack(nc, x, adj_cols, adj_mask, w_self, w_neigh, b0, t1, bt1, w11, b11, w12, b12,
              w_hyp, b_hyp, w_dec, b_dec, out):
    fp32, bf16, i16 = mybir.dt.float32, mybir.dt.bfloat16, mybir.dt.int16
    ALU, ACT = mybir.AluOpType, mybir.ActivationFunctionType
    AX = mybir.AxisListType.X
    ctx = ExitStack()
    with ctx:
        cursor = [(nc.sbuf_base + 63) // 64 * 64]

        def place(name, shape, dt=fp32):
            n = 1
            for s in shape[1:]:
                n *= s
            at = cursor[0]
            cursor[0] = at + (n * mybir.dt.size(dt) + 31) // 32 * 32
            return nc.alloc_sbuf_tensor_at(name, shape, dt, offset=at)

        def sem(name):
            return ctx.enter_context(nc.semaphore(name))

        ident = place("ident", [P, P])
        counts = place("counts", [P, NB, NB], bf16)
        deg = place("deg", [P, NB])
        base = place("base", [P, NB, D])
        small = place("small", [P, 16, 2])
        rows = place("rows", [P, 2, SPL])
        t_a = place("t_a", [P, 2, D])
        t_b = place("t_b", [P, 2, D])
        t_c = place("t_c", [P, 2, D])
        kept = cursor[0]
        z_spl = place("z_spl", [P, NB, SPL + NB], bf16)
        w0 = place("w0", [NW, 2 * D])
        w1u = place("w1u", [NW, 2 * D])
        w1h = place("w1h", [D, HID])
        t_rows = rows[0:2, 0, 0:HID]
        t_one = place("t_one", [2, 1])
        bias11 = place("bias11", [HID, 1])
        w1o = place("w1o", [HID, D])
        x_in = place("x_in", [P, 3, 2, D])
        hT = place("hT", [NW, CW])
        hidT = place("hidT", [HID, CW])
        ux_in = place("ux_in", [P, 2, 2 * D])
        xb_spl = place("xb_spl", [P, NB, SPL], bf16)
        adj_at = cursor[0]
        adj = place("adj", [P, NC, NB * CW], bf16)
        cursor[0] -= 2 * NB * CW * mybir.dt.size(bf16)
        x_all = place("x_all", [P, NB, D])
        h_quad = place("h_quad", [P, 2, 4, D])
        hT4 = place("hT4", [NW, 2, 4 * P])
        r_quad = place("r_quad", [P, 4, D])
        sq_all = place("sq_all", [P, NB, D])
        st_all = place("st_all", [P, 4, NB])
        cursor[0] = kept
        h2 = place("h2", [P, NB, D])
        pick_b = place("pick_b", [KN, P], bf16)
        norms = place("norms", [P, NB, 10], bf16)
        w2h = place("w2h", [D, D])
        b2_all = place("b2_all", [P, D])
        w3d = place("w3d", [D, D])
        b3_all = place("b3_all", [P, D])
        zero_row = place("zero_row", [1, 512], bf16)
        ident16 = place("ident16", [P, P], bf16)
        order = place("order", [P, P], bf16)
        row_quad = place("row_quad", [P, 2, 4, D])
        featT = place("featT", [D, 2, 4 * P])
        t_quad = place("t_quad", [P, 4, D])
        x2 = place("x2", [P, NB])
        x_b = place("x_b", [P, NB])
        pn = place("pn", [P, 8, NB])
        late = cursor[0]
        assert late <= nc.sbuf_base + 63 + 40000
        parts = nc.alloc_sbuf_tensor_at("parts", [P, NB, TURNS * D], bf16, offset=adj_at)
        assert late <= adj_at and NB * TURNS * D <= 2 * NB * CW
        UW = [n * P for n in UB]
        gain = [place(f"gain{k}", [P, UW[k % 2]]) for k in range(4)]
        nrm = [place(f"nrm{u}", [P, UW[u]]) for u in range(2)]
        atanh = [place(f"atanh{u}", [P, UW[u]]) for u in range(2)]
        den = place("den", [P, UW[0]])
        dist = [place(f"dist{k}", [P, UW[k]]) for k in range(2)]
        p_dir = [place(f"p_dir{u}", [P, UW[u]]) for u in range(2)]
        p_tr = [place(f"p_tr{u}", [P, 6 * P]) for u in range(2)]
        xrow = place("xrow", [P, EXB, NW])
        own = place("own", [P, NB, 3, P], bf16)
        far12 = place("far12", [P, EXB * P], bf16)
        far31 = place("far31", [P, EXB * P], bf16)
        own_n = place("own_n", [KN, NP], bf16)
        far_n = place("far_n", [KN, EXB * P], bf16)
        x_b_row = place("x_b_row", [P, EXB * P])
        mask = [[place(f"mask{u}{k}", [P, UW[u] + 6 * P]) for k in range(2)] for u in range(2)]
        behind3 = cursor[0]
        adj4 = [place("adj4_0", [P, NB * CW], bf16)]
        assert cursor[0] <= nc.sbuf_usable_end, cursor
        cursor[0] = late
        adj4.append(place("adj4_1", [P, NB * CW], bf16))
        w_exp = [place(f"w_exp{k}", [P, NB, CW], i16) for k in range(2)]
        o_buf = place("o_buf", [P, 2, 2, D])
        s_spl = place("s_spl", [P, NB, SPL], bf16)
        countsT = place("countsT", [NB, NP], bf16)
        later = place("later", [NB, NB, P], bf16)
        post = [place(f"post{k}", [P, NB, D]) for k in range(4)]
        assert cursor[0] <= behind3

        lo = ctx.enter_context(nc.psum_tensor("lo", [P, 2048], fp32))
        hi = ctx.enter_context(nc.psum_tensor("hi", [P, 2048], fp32))
        agg = lo[:, :].rearrange("p (b n) -> p b n", b=4)
        tp = hi[:, 0:512]
        mm = hi[:, 512:1024]
        ux = hi[:, 1024:1536].rearrange("p (b n) -> p b n", b=2)
        one = hi[:, 1536:2048]
        ux_bank = hi[:, 1024:1536]
        side_ps = [b.rearrange("p (b k n) -> p b k n", b=2, k=2) for b in (tp, mm)]
        dist_ps = hi[:, 0:1024]
        turn_ps = hi[:, 1024:2048].rearrange("p (k n) -> p k n", k=2)
        exp_ps = [hi[:, 0:1024], hi[:, 1024:2048]]


        def acc_at(j):
            return j * 72 + j // 7 * 8

        x_in_sem = [sem(f"x_loaded{k}") for k in range(3)]
        x_all_loaded = sem("x_all_loaded")
        weights_loaded = sem("weights_loaded")
        adj_loaded = [sem(f"adj_loaded{k}") for k in range(2)]
        consts_made = sem("consts_made")
        dve_step = sem("dve_step")
        act_step = sem("act_step")
        pool_step = sem("pool_step")
        var_ready = sem("var_ready")
        root_ready = sem("root_ready")
        h_ready = sem("h_ready")
        turned = sem("turned")
        hT_ready = sem("hT_ready")
        z_ready = sem("z_ready")
        z_split = sem("z_split")
        agg_ready = sem("agg_ready")
        agg_read = sem("agg_read")
        hid_ready = sem("hid_ready")
        tanh_ready = sem("tanh_ready")
        ux_ready = sem("ux_ready")
        base_ready = sem("base_ready")
        bias_ps_ready = sem("bias_ps_ready")
        bias_ready = sem("bias_ready")
        rows_made = sem("rows_made")
        h2_ready = sem("h2_ready")
        x2_ready = sem("x2_ready")
        ux_copied = sem("ux_copied")
        STEPS1, STEPS2 = 16, 7
        mask_loaded = [[sem(f"mask_loaded{u}{k}") for k in range(2)] for u in range(2)]
        late_loaded = sem("late_loaded")
        late_made = sem("late_made")
        parts_ready = sem("parts_ready")
        parts_copied = sem("parts_copied")
        parts_turned = sem("parts_turned")
        own_copied = sem("own_copied")
        far_copied = sem("far_copied")
        norms_ready = sem("norms_ready")
        norms_turned = sem("norms_turned")
        far_n_copied = sem("far_n_copied")
        own_n_copied = sem("own_n_copied")
        row_ready = sem("row_ready")
        row_copied = [sem(f"row_copied{k}") for k in range(2)]
        xrow_ready = sem("xrow_ready")
        wrapped = sem("wrapped")
        dist_ready = sem("dist_ready")
        apart = sem("apart")
        prod_ready = sem("prod_ready")
        inv_ready = sem("inv_ready")
        nrm_ready = sem("nrm_ready")
        logs_ready = sem("logs_ready")
        atanh_ready = sem("atanh_ready")
        gain_ready = sem("gain_ready")
        dir_ready = [sem(f"dir_ready{u}") for u in range(2)]
        turn_ready = sem("turn_ready")
        tr_ready = sem("tr_ready")
        dir_used = sem("dir_used")
        tr_used = sem("tr_used")
        quad_ready = sem("quad_ready")
        quad_turned = sem("quad_turned")
        feat_ready = sem("feat_ready")
        sums_read = sem("sums_read")
        lin_ready = sem("lin_ready")
        lin_read = sem("lin_read")
        x3_ready = sem("x3_ready")
        bias_added = sem("bias_added")
        counts_turned = sem("counts_turned")
        counts_copied = sem("counts_copied")
        nv_ready = sem("nv_ready")
        tanh3_ready = sem("tanh3_ready")
        adj4_loaded = [sem(f"adj4_loaded{k}") for k in range(2)]
        exps_made = [sem(f"exps_made{k}") for k in range(2)]
        exps_read = [sem(f"exps_read{k}") for k in range(2)]
        out_made = sem("out_made")
        out_sent = [sem(f"out_sent{k}") for k in range(2)]
        block = ctx.enter_context(nc.Block())

        class Chain:

            def __init__(self, eng, s):
                self.eng, self.s, self.n, self.base = eng, s, 0, 0

            def __call__(self, ins):
                ins.then_inc(self.s, 1)
                self.n += 1
                self.eng.wait_ge(self.s, self.base + self.n)

            def go(self, ins):
                ins.then_inc(self.s, 1)
                self.n += 1

            def turn(self, start, index, steps):
                self.base, self.n = start + index * steps, 0

        def each_pair(eng, body):
            body(0, 0)
            body(1, 1)
            with eng.Fori(2, NC - 1, 2) as c:
                body(c, 0)
                body(c + 1, 1)
            body(NC - 1, 0)

        UNITS = 4 * NC
        QUADS = [(j, min(4, NB - j)) for j in range(0, NB, 4)]
        NQ = len(QUADS)
        NORMS_AT = NC - NQ
        GROUP = [(j, min(4, NB - j)) for j in range(0, NB, 4)]
        GROUPS = ((len(GROUP) + 1) // 2, len(GROUP) // 2)
        W_SHIFT = 128.0 * HORIZON - EDGE

        def wide(v, n=D):
            return v.unsqueeze(2).broadcast_to([P, v.shape[1], n])

        def pair(t, c):
            return t[:, bass.ds(2 * c, 2)]

        @block.sync
        def _(sp):
            sp.dma_start(x_all[:, :, :], x).then_inc(x_all_loaded, 16)
            sp.dma_start(w0[0:D, 0:D], w_self).then_inc(weights_loaded, 16)
            sp.dma_start(w0[0:D, D:2 * D], w_neigh).then_inc(weights_loaded, 16)
            sp.dma_start(w0[D:NW, 0:D], b0).then_inc(weights_loaded, 16)
            sp.dma_start(w1u[0:D, 0:D], bt1).then_inc(weights_loaded, 16)
            sp.dma_start(w1h[:, :], w11[0:D, :]).then_inc(weights_loaded, 16)
            sp.dma_start(t_rows[0:1], w11[D:NW, :]).then_inc(weights_loaded, 16)
            sp.dma_start(t_rows[1:2], b11).then_inc(weights_loaded, 16)
            sp.dma_start(t_one[:, :], t1).then_inc(weights_loaded, 16)
            sp.dma_start(w1o[:, :], w12).then_inc(weights_loaded, 16)
            sp.dma_start(w1u[D:NW, D:2 * D], b12).then_inc(weights_loaded, 16)

            for c in range(NC):
                if c >= 3:
                    sp.wait_ge(base_ready, c - 2)
                sp.dma_start(x_in[:, c % 3], pair(x, c)).then_inc(x_in_sem[c % 3], 16)

            sp.wait_ge(h2_ready, NC)
            sp.dma_start(w2h[:, :], w_hyp).then_inc(late_loaded, 16)
            sp.dma_start(b2_all[:, :], b_hyp.broadcast_to([P, D])).then_inc(late_loaded, 16)
            sp.dma_start(w3d[:, :], w_dec).then_inc(late_loaded, 16)
            sp.dma_start(b3_all[:, :], b_dec.broadcast_to([P, D])).then_inc(late_loaded, 16)

            def load_mask(i, r, u, s):
                if not isinstance(s, int) or s >= 1:
                    sp.wait_ge(tr_ready, 2 * (4 * s + 2 * r + u) - 6)
                    sp.wait_ge(dir_ready[u], 2 * s + r - 1)
                at = u * (UW[0] + 6 * P)
                sp.dma_start(mask[u][r][:, :], adj_mask[i, :, at:at + UW[u] + 6 * P]) \
                    .then_inc(mask_loaded[u][r], 16)

            for r in range(2):
                for u in range(2):
                    load_mask(r, r, u, 0)
            with sp.Fori(1, NC) as s:
                for r in range(2):
                    for u in range(2):
                        load_mask(2 * s + r, r, u, s)

            def send(c, q):
                sp.wait_ge(out_made, c + 1)
                sp.dma_start(pair(out, c), o_buf[:, q]).then_inc(out_sent[q], 16)

            each_pair(sp, send)
            sp.wait_ge(out_sent[0], (NC + 1) // 2 * 16)
            sp.wait_ge(out_sent[1], NC // 2 * 16)

        @block.gpsimd
        def _(pool):
            def load_adj(c, q):
                pool.dma_start(adj[:, c], adj_cols[c]).then_inc(adj_loaded[q], 16)

            load_adj(0, 0)
            load_adj(1, 1)
            step = Chain(pool, pool_step)
            step(pool.memset(ident[:, :], 0.0))
            pool.affine_select(out=ident[:, :], in_=ident[:, :], compare_op=ALU.not_equal, fill=1.0,
                               base=0, pattern=[[-1, P]], channel_multiplier=1).then_inc(consts_made, 1)
            hot = z_spl[:, :, SPL:SPL + NB]
            step(pool.memset(hot, 0.0))
            pool.affine_select(out=hot, in_=hot, compare_op=ALU.not_equal, fill=1.0,
                                    base=0, pattern=[[1, NB], [-1, NB]], channel_multiplier=0).then_inc(consts_made, 1)

            def next_adj(c, q):
                pool.wait_ge(adj_loaded[q], (c // 2) * 16)
                load_adj(c, q)

            with pool.Fori(2, NC - 3, 2) as c:
                next_adj(c, 0)
                next_adj(c + 1, 1)
            next_adj(NC - 3, 0)
            pool.wait_ge(z_split, NQ)
            next_adj(NC - 2, 1)
            next_adj(NC - 1, 0)

            def residual(c):
                pool.wait_ge(ux_copied, c + 1)
                xb, u, parts, x2 = ux_in[:, :, 0:D], ux_in[:, :, D:2 * D], pair(xb_spl, c), pair(base, c)
                step.go(pool.tensor_copy(parts[:, :, 0:D], xb))
                step(pool.tensor_tensor(x2, xb, wide(deg[:, bass.ds(2 * c, 2)]), ALU.mult))
                step.go(pool.tensor_tensor(xb, xb, parts[:, :, 0:D], ALU.subtract))
                step(pool.tensor_tensor(x2, x_in[:, c % 3], x2, ALU.subtract))
                step(pool.tensor_copy(parts[:, :, D:2 * D], xb))
                step(pool.tensor_tensor(parts[:, :, 2 * D:SPL], xb, parts[:, :, D:2 * D], ALU.subtract))
                pool.tensor_tensor(x2, x2, u, ALU.add).then_inc(base_ready, 1)

            for c in range(NC):
                residual(c)

            pool.wait_ge(agg_ready, NC)
            step(pool.memset(ident16[:, :], 0.0))
            pool.affine_select(out=ident16[:, :], in_=ident16[:, :], compare_op=ALU.not_equal, fill=1.0,
                               base=0, pattern=[[-1, P]], channel_multiplier=1).then_inc(late_made, 1)
            step(pool.memset(order[:, :], 0.0))
            step(pool.affine_select(out=order[:, :], in_=order[:, :], compare_op=ALU.is_ge, fill=-128.0,
                                    base=0, pattern=[[1, P]], channel_multiplier=-1))
            pool.affine_select(out=order[:, :], in_=order[:, :], compare_op=ALU.not_equal, fill=EDGE,
                               base=0, pattern=[[-1, P]], channel_multiplier=1).then_inc(late_made, 1)
            step(pool.memset(pick_b[:, :], 0.0))
            step(pool.affine_select(out=pick_b[:, :], in_=pick_b[:, :], compare_op=ALU.is_ge, fill=-1.0,
                                    base=-3, pattern=[[0, P]], channel_multiplier=1))
            pool.affine_select(out=pick_b[:, :], in_=pick_b[:, :], compare_op=ALU.not_equal, fill=1.0,
                               base=-3, pattern=[[0, P]], channel_multiplier=1).then_inc(late_made, 1)

            def split_rows(c):
                pool.wait_ge(h2_ready, c + 1)
                v, rest, got = pair(h2, c), rows[:, :, 0:D], pair(parts, c)
                part = [got[:, :, k * D:(k + 1) * D] for k in range(TURNS)]
                step(pool.tensor_copy(part[5], v))
                step(pool.tensor_tensor(rest, v, part[5], ALU.subtract))
                step(pool.tensor_copy(part[6], rest))
                pool.tensor_tensor(part[4], rest, part[6], ALU.subtract).then_inc(parts_ready, 1)
                pool.wait_ge(parts_ready, c + 1)

            pool.wait_ge(agg_ready, NC + 2)
            for c in range(NC):
                split_rows(c)
            pool.wait_ge(h2_ready, NC)
            pool.tensor_copy(xrow[:, 0:NB, 0:D], h2[:, :, :]).then_inc(xrow_ready, 1)
            pool.tensor_copy(xrow[:, NB:EXB, 0:D], h2[:, 0:EXB - NB, :]).then_inc(xrow_ready, 1)

            def norm(t, k):
                if not isinstance(t, int) or t >= 2:
                    pool.wait_ge(atanh_ready, t - 1)
                pool.wait_ge(inv_ready, t + 1)
                pool.tensor_tensor(nrm[k % 2][:, :], dist[k % 2][:, :], gain[k][:, :], ALU.mult).then_inc(nrm_ready, 1)

            def twice_atanh(t, k):
                u = k % 2
                pool.wait_ge(logs_ready, t + 1)
                pool.tensor_tensor(atanh[u][:, :], atanh[u][:, :], nrm[u][:, :], ALU.subtract) \
                    .then_inc(atanh_ready, 1)

            def masked(s, r):
                t = 4 * s + 2 * r
                pool.wait_ge(gain_ready, t + 1)
                pool.wait_ge(mask_loaded[0][r], 16 * s + 16)
                if not isinstance(t, int) or t >= 2:
                    pool.wait_ge(dir_used, t - 1)
                pool.tensor_tensor(p_dir[0][:, :], gain[2 * r][:, :], mask[0][r][:, 0:UW[0]], ALU.mult) \
                    .then_inc(dir_ready[0], 1)

            def units(s):
                for k in range(4):
                    t = 4 * s + k
                    if not isinstance(t, int) or t >= 1:
                        norm(t - 1, (k - 1) % 4)
                    if not isinstance(t, int) or t >= 2:
                        twice_atanh(t - 2, (k - 2) % 4)
                    if k == 1 and (not isinstance(s, int) or s >= 1):
                        masked(s - 1, 1)
                    elif k == 3:
                        masked(s, 0)

            def load_adj4(c, q):
                pool.dma_start(adj4[q][:, :], adj_cols[c]).then_inc(adj4_loaded[q], 16)

            load_adj4(0, 0)
            units(0)
            with pool.Fori(1, NC) as s:
                units(s)
            norm(UNITS - 1, 3)
            twice_atanh(UNITS - 2, 2)
            masked(NC - 1, 1)
            twice_atanh(UNITS - 1, 3)
            pool.wait_ge(tr_used, UNITS)
            load_adj4(1, 1)
            step(pool.memset(later[:, :, :], 0.0))
            pool.affine_select(out=later[:, :, :], in_=later[:, :, :], compare_op=ALU.is_ge, fill=-128.0,
                               base=0, pattern=[[1, NB], [0, P]], channel_multiplier=-1).then_inc(late_made, 1)


            pool.wait_ge(var_ready, 3 * NC + 3)
            pool.wait_ge(late_loaded, 64)
            pool.tensor_tensor(base[:, :, :], base[:, :, :], b3_all[:, :].unsqueeze(1).broadcast_to([P, NB, D]),
                               ALU.add).then_inc(bias_added, 1)

            def next_adj4(c, q):
                pool.wait_ge(exps_made[0], GROUPS[0] * (c - 1))
                pool.wait_ge(exps_made[1], GROUPS[1] * (c - 1))
                load_adj4(c, q)

            with pool.Fori(2, NC - 1, 2) as c:
                next_adj4(c, 0)
                next_adj4(c + 1, 1)
            next_adj4(NC - 1, 0)

        @block.scalar
        def _(act):
            step = Chain(act, act_step)

            def root(n, dst, src):
                act.wait_ge(var_ready, n + 1)
                act.activation(dst, src, ACT.Sqrt).then_inc(root_ready, 1)

            def deviation(n, dst, src):
                act.wait_ge(var_ready, n + 1)
                act.activation(dst, src, ACT.Sqrt, scale=1.0 / D, bias=EPS).then_inc(root_ready, 1)

            deviation(0, st_all[:, 2, :], st_all[:, 1, :])
            act.wait_ge(bias_ps_ready, 1)
            act.activation(bias11[:, :], one[:, 0:1], ACT.Copy).then_inc(bias_ready, 1)

            def copy_hT(c):
                act.wait_ge(turned, NQ + c + 1)
                act.activation(hT[0:D, :], tp[0:D, 0:CW], ACT.Copy).then_inc(hT_ready, 1)

            for i, (j, n) in enumerate(QUADS):
                act.wait_ge(turned, i + 1)
                if i >= 2:
                    act.wait_ge(z_ready, i - 1)
                act.activation(hT4[0:D, i % 2, 0:n * P], (tp, ux_bank)[i % 2][0:D, 0:n * P], ACT.Copy) \
                    .then_inc(hT_ready, 1)

            for k in range(NC + 1):
                c = k - 1
                if c >= 0:
                    copy_hT(c)
                if k < NC:
                    root(2 * k + 1, small[:, 4, :], small[:, 3, :])
                if c >= 0:
                    act.wait_ge(hid_ready, c + 1)
                    act.activation(hidT[:, :], mm[:, 0:CW], ACT.Tanh, bias=bias11[:, :]).then_inc(tanh_ready, 1)
                if k < NC:
                    deviation(2 * k + 2, small[:, 9, :], small[:, 8, :])
                if c >= 0:
                    act.wait_ge(ux_ready, c + 1)
                    if c >= 1:
                        act.wait_ge(base_ready, c)
                    act.activation(ux_in[:, :, :], ux[:, :, 0:2 * D], ACT.Copy).then_inc(ux_copied, 1)

            AHEAD = NC - 4

            def copy_parts(c):
                act.wait_ge(parts_ready, c + 1)
                got = pair(parts, c)
                for to, part in ((2, 5), (0, 6)):
                    ins = act.activation(got[:, :, to * D:(to + 2) * D].rearrange("p b (k d) -> p b k d", k=2),
                                         got[:, :, part * D:(part + 1) * D].unsqueeze(2)
                                         .broadcast_to([P, 2, 2, D]), ACT.Copy)
                ins.then_inc(parts_copied, 1)

            for c in range(NC):
                deviation(2 * NC + 1 + c, small[:, 9, :], small[:, 8, :])
                if c >= NC - AHEAD:
                    copy_parts(c - NC + AHEAD)
            def copy_own(c):
                act.wait_ge(parts_turned, c + 1)
                act.activation(pair(own, c).rearrange("p b k n -> p b (k n)"),
                               agg[:, c % 2 * 2:c % 2 * 2 + 2, 0:3 * P], ACT.Copy, scale=-2.0).then_inc(own_copied, 1)

            def copy_far_n(k):
                j, n = QUADS[k]
                act.wait_ge(norms_turned, k + 1)
                act.activation(far_n[:, j * P:(j + n) * P], ux_bank[0:KN, 0:n * P], ACT.Copy) \
                    .then_inc(far_n_copied, 1)

            act.wait_ge(h2_ready, NC)
            for c in range(NC):
                copy_own(c)
                if c + AHEAD < NC:
                    copy_parts(c + AHEAD)
                if c >= NORMS_AT:
                    copy_far_n(c - NORMS_AT)
            for k in range(0, NQ, 2):
                j, n = QUADS[k]
                act.wait_ge(row_ready, k + 1)
                act.activation(x_b_row[:, j * P:(j + n) * P], agg[:, k % 4, 0:n * P], ACT.Copy) \
                    .then_inc(row_copied[0], 1)
            act.preload_act_table_set("natural_log_exp_and_others")

            def inverse(t, k):
                act.wait_ge(prod_ready, t + 1)
                step(act.activation(gain[k][:, :], gain[k][:, :], ACT.Ln, bias=LN_FLOOR))
                act.activation(gain[k][:, :], gain[k][:, :], ACT.Exp, scale=-0.5).then_inc(inv_ready, 1)

            def logs(t, k):
                u = k % 2
                act.wait_ge(nrm_ready, t + 1)
                step(act.activation(nrm[u][:, :], nrm[u][:, :], ACT.Relu, scale=-1.0, bias=TANH_CLIP))
                if not isinstance(t, int) or t >= 2:
                    act.wait_ge(gain_ready, t - 1)
                act.activation(atanh[u][:, :], nrm[u][:, :], ACT.Ln, scale=-1.0, bias=1.0 + TANH_CLIP)
                act.activation(nrm[u][:, :], nrm[u][:, :], ACT.Ln, bias=1.0 - TANH_CLIP).then_inc(logs_ready, 1)

            def units(s):
                for r in range(2):
                    for u in range(2):
                        k = 2 * r + u
                        t = 4 * s + k
                        step.turn(act3, t, 2)
                        if isinstance(t, int) and t == 0:
                            step.n = 1
                        inverse(t, k)
                        if not isinstance(t, int) or t >= 1:
                            logs(t - 1, (k - 1) % 4)

            act3 = step.n - 1
            units(0)
            with act.Fori(1, NC) as s:
                units(s)
            step.turn(act3, UNITS, 2)
            step.n = 0
            logs(UNITS - 1, 3)

            def copy_feat(i):
                w = QUADS[i % NQ][1] * P
                act.wait_ge(quad_turned, i + 1)
                if i >= 2:
                    act.wait_ge(lin_ready, i - 1)
                act.activation(featT[:, i % 2, 0:w], (tp, ux_bank)[i % 2][0:D, 0:w], ACT.Copy) \
                    .then_inc(feat_ready, 1)

            for k, (j, n) in enumerate(QUADS):
                act.wait_ge(counts_turned, k + 1)
                act.activation(countsT[:, j * P:(j + n) * P], agg[0:NB, k % 2, 0:n * P], ACT.Copy) \
                    .then_inc(counts_copied, 1)
            for i in range(NQ):
                copy_feat(i)
            root(3 * NC + 1, pn[:, 6, :], pn[:, 5, :])
            act.wait_ge(nv_ready, 1)
            act.activation(pn[:, 7, :], pn[:, 6, :], ACT.Tanh).then_inc(tanh3_ready, 1)

            def group_weights(c, q, g):
                (j, n), k = GROUP[g], g % 2
                act.wait_ge(exps_made[k], GROUPS[k] * c + g // 2 + 1)
                if g == 0 and (not isinstance(c, int) or c >= 2):
                    act.wait_ge(agg_ready, 2 * NC + c - 1)
                act.activation(w_exp[q][:, j:j + n, :].rearrange("p j n -> p (j n)"),
                               exp_ps[k][:, 0:n * CW], ACT.Relu, bias=W_SHIFT).then_inc(exps_read[k], 1)

            for g in range(len(GROUP)):
                group_weights(0, 0, g)
            deviation(3 * NC + 2, pn[:, 2, :], pn[:, 3, :])
            for i in range(NQ, 2 * NQ):
                copy_feat(i)

            def weights(c, q):
                for g in range(0, len(GROUP), 2):
                    group_weights(c, q, g)

            weights(1, 1)
            with act.Fori(2, NC - 1, 2) as c:
                weights(c, 0)
                weights(c + 1, 1)
            weights(NC - 1, 0)

        @block.tensor
        def _(pe):
            pe.wait_ge(weights_loaded, 160)
            pe.wait_ge(consts_made, 2)
            pe.wait_ge(rows_made, 5)
            pe.matmul(one[:, 0:1], t_rows, t_one[:, :], start=True, stop=True).then_inc(bias_ps_ready, 1)

            def turn_pair(c):
                pe.wait_ge(h_ready, NQ + c + 1)
                pe.wait_ge(hT_ready, NQ + c)
                for b in range(2):
                    ins = pe.matmul(tp[0:D, b * P:(b + 1) * P], t_c[:, b, :], ident[:, :], start=True, stop=True)
                ins.then_inc(turned, 1)

            def turn_first(i):
                pe.wait_ge(h_ready, i + 1)
                if i >= 2:
                    pe.wait_ge(hT_ready, i - 1)
                for m in range(QUADS[i][1]):
                    ins = pe.transpose((tp, ux_bank)[i % 2][0:D, m * P:(m + 1) * P], h_quad[:, i % 2, m, :],
                                       ident[:, :])
                ins.then_inc(turned, 1)

            pe.wait_ge(bias_ready, 1)
            turn_first(0)
            for i in range(NQ):
                if i + 1 < NQ:
                    turn_first(i + 1)
                pe.wait_ge(hT_ready, i + 1)
                if i >= 2:
                    pe.wait_ge(z_split, i - 1)
                for m in range(QUADS[i][1]):
                    ins = pe.matmul((mm, one)[i % 2][:, m * P:(m + 1) * P], hT4[:, i % 2, m * P:(m + 1) * P],
                                    w0[:, :], start=True, stop=True)
                ins.then_inc(z_ready, 1)

            def gather(c, b, n, terms, width, first=0, last=NB):
                if b == 0 and first == 0 and n >= 2:
                    pe.wait_ge(agg_read, n - 1)
                for j in range(first, last):
                    ins = pe.matmul(agg[:, n % 2 * 2 + b, 0:width],
                                    adj[:, c, j * CW + b * P:j * CW + (b + 1) * P],
                                    terms[:, j, 0:width], start=(j == 0), stop=(j == NB - 1))
                if b == 1 and last == NB:
                    ins.then_inc(agg_ready, 1)

            EARLY = NC - 3
            pe.wait_ge(z_split, NQ)
            for k in range(NC + 2):
                c = k - 2
                if c >= 0:
                    turn_pair(c)
                if k < NC:
                    pe.wait_ge(adj_loaded[k % 2], (k // 2 + 1) * 16)
                    gather(k, 0, k, z_spl, SPL + NB)
                else:
                    pe.wait_ge(base_ready, EARLY)
                    gather(k - NC, 0, k, xb_spl, SPL, 0, 2 * EARLY)
                if c >= 0:
                    pe.wait_ge(hT_ready, NQ + c + 1)
                    if c >= 1:
                        pe.wait_ge(ux_copied, c)
                        pe.wait_ge(tanh_ready, c)
                    pe.matmul(mm[:, 0:CW], w1h[:, :], hT[0:D, :], start=True, stop=True).then_inc(hid_ready, 1)
                    for b in range(2):
                        pe.matmul(ux[:, b, 0:2 * D], hT[:, b * P:(b + 1) * P], w1u[:, :], start=b == 0, stop=False,
                                  skip_group_check=True)
                if k < NC:
                    gather(k, 1, k, z_spl, SPL + NB)
                else:
                    gather(k - NC, 1, k, xb_spl, SPL, 0, 2 * EARLY)
                if c >= 0:
                    pe.wait_ge(tanh_ready, c + 1)
                    for b in range(2):
                        ins = pe.matmul(ux[:, b, D:2 * D], hidT[:, b * P:(b + 1) * P], w1o[:, :],
                                        start=False, stop=b == 1, skip_group_check=True)
                    ins.then_inc(ux_ready, 1)
            pe.wait_ge(base_ready, NC)

            for c in range(NC):
                for b in range(2):
                    gather(c, b, NC + c, xb_spl, SPL, 2 * EARLY if c < 2 else 0)


            pe.wait_ge(late_made, 3)
            pe.wait_ge(agg_read, 2 * NC)

            def distances(s, r, u):
                t = 4 * s + 2 * r + u
                if t >= 1:
                    pe.wait_ge(apart, t)
                i = 2 * s + r
                for k, (w, v) in enumerate(((own[:, i, 0, :], far12), (own[:, i, 1, :], far12),
                                            (own[:, i, 2, :], far31), (own_n[:, i * P:(i + 1) * P], far_n))):
                    for at in range(0, UW[u], 512):
                        n = min(512, UW[u] - at)
                        col = s * CW + UO[u] * P + at
                        ins = pe.matmul(dist_ps[:, at:at + n], w, v[:, col:col + n], start=k == 0, stop=k == 3)
                ins.then_inc(dist_ready, 1)

            def turn_norms(k):
                j, n = QUADS[k]
                pe.wait_ge(norms_ready, 1)
                if k >= 1:
                    pe.wait_ge(far_n_copied, k)
                    pe.wait_ge(own_n_copied, k)
                for first, bank in ((0, ux_bank), (3, one)):
                    for m in range(n):
                        ins = pe.matmul(bank[0:KN, m * P:(m + 1) * P], norms[:, j + m, first:first + KN],
                                        ident16[:, :], start=True, stop=True)
                ins.then_inc(norms_turned, 1)

            for c in range(NC):
                pe.wait_ge(parts_ready, c + 1)
                pe.wait_ge(parts_copied, c + 1)
                if c >= 2:
                    pe.wait_ge(own_copied, c - 1)
                    pe.wait_ge(far_copied, c - 1)
                for b in range(2):
                    i = 2 * c + b
                    for k, first in enumerate((0, 2, 3)):
                        pe.matmul(agg[:, c % 2 * 2 + b, k * P:(k + 1) * P],
                                  parts[:, i, first * D:first * D + P], ident16[:, :], start=True, stop=True)
                    for k, first in enumerate((5, 4)):
                        ins = pe.matmul(side_ps[c % 2][:, b, k, :], parts[:, i, first * D:first * D + P],
                                        ident16[:, :], start=True, stop=True)
                ins.then_inc(parts_turned, 1)
                if c >= NORMS_AT:
                    turn_norms(c - NORMS_AT)
            pe.wait_ge(own_copied, NC)
            pe.wait_ge(far_copied, NC)
            pe.wait_ge(far_n_copied, NQ)
            pe.wait_ge(own_n_copied, NQ)
            distances(0, 0, 0)
            for k, (j, n) in enumerate(QUADS):
                pe.wait_ge(far_n_copied, k + 1)
                if k >= 4:
                    pe.wait_ge(row_copied[k % 2], (k - 4) // 2 + 1)
                pe.matmul(agg[:, k % 4, 0:n * P], pick_b[:, :], far_n[:, j * P:(j + n) * P],
                          start=True, stop=True).then_inc(row_ready, 1)
            pe.wait_ge(row_copied[0], (NQ + 1) // 2)
            pe.wait_ge(row_copied[1], NQ // 2)
            for b in range(4):
                pe.matmul(agg[:, b, :], zero_row[:, 0:P], zero_row[:, :], start=True, stop=False,
                          skip_group_check=True)
            def turn_gains(s, r, u):
                t = 4 * s + 2 * r + u
                pe.wait_ge(gain_ready, t + 1)
                for h in range(2):
                    if t >= 1:
                        pe.wait_ge(tr_ready, 2 * t - 1 + h)
                    for k in range(3):
                        at = (UT[u] - UO[u] + 3 * h + k) * P
                        ins = pe.transpose(turn_ps[:, h, k * P:(k + 1) * P], gain[2 * r + u][:, at:at + P],
                                           ident[:, :])
                    ins.then_inc(turn_ready, 1)

            def sums(s, r, u):
                pe.wait_ge(dir_ready[u], 2 * s + r + 1)
                for k in range(UB[u]):
                    at = acc_at((2 * s + UO[u] + k) % NB)
                    ins = pe.matmul(lo[:, at:at + NW], p_dir[u][:, k * P:(k + 1) * P],
                                    xrow[:, 2 * s + r, :], start=False, stop=False, skip_group_check=True)
                ins.then_inc(dir_used, 1)

            def sums_turned(s, r, u):
                at = acc_at(2 * s + r)
                for h in range(2):
                    pe.wait_ge(tr_ready, 2 * (4 * s + 2 * r + u) + 1 + h)
                    for k in range(3):
                        m = 3 * h + k
                        ins = pe.matmul(lo[:, at:at + NW], p_tr[u][:, m * P:(m + 1) * P],
                                        xrow[:, 2 * s + UT[u] + m, :], start=False, stop=False,
                                        skip_group_check=True)
                ins.then_inc(tr_used, 1)

            def hold_clock(n):
                idle_cols = counts[:, :, :].rearrange("p a b -> p (a b)")[:, 0:512]
                for _ in range(n):
                    pe.matmul(tp[:, :], ident16[:, :], idle_cols, start=True, stop=True)

            order_of = [(s, r, u) for s in range(NC) for r in range(2) for u in range(2)]
            for t in range(UNITS + 4):
                if t == 3:
                    pe.wait_ge(wrapped, 5)
                if t == UNITS:
                    pe.wait_ge(apart, UNITS)
                    hold_clock(8)
                if t + 1 < UNITS:
                    distances(*order_of[t + 1])
                if t >= 4:
                    sums(*order_of[t - 4])
                    sums_turned(*order_of[t - 4])
                if 3 <= t < UNITS + 3:
                    turn_gains(*order_of[t - 3])
            pe.wait_ge(late_loaded, 64)

            pe.wait_ge(sums_read, 1)
            for k, (j, n) in enumerate(QUADS):
                if k >= 2:
                    pe.wait_ge(counts_copied, k - 1)
                for m in range(n):
                    ins = pe.matmul(agg[0:NB, k % 2, m * P:(m + 1) * P], counts[:, j + m, :],
                                    ident16[:, :], start=True, stop=True)
                ins.then_inc(counts_turned, 1)

            def turn_quad(i):
                pe.wait_ge(quad_ready, i + 1)
                if i >= 2:
                    pe.wait_ge(feat_ready, i - 1)
                for m in range(QUADS[i % NQ][1]):
                    ins = pe.transpose((tp, ux_bank)[i % 2][0:D, m * P:(m + 1) * P], row_quad[:, i % 2, m, :],
                                       ident[:, :])
                ins.then_inc(quad_turned, 1)

            def linear(i, w):
                pe.wait_ge(feat_ready, i + 1)
                if i >= 2:
                    pe.wait_ge(lin_read, i - 1)
                for m in range(QUADS[i % NQ][1]):
                    ins = pe.matmul((mm, one)[i % 2][:, m * D:(m + 1) * D], featT[:, i % 2, m * P:(m + 1) * P],
                                    w[:, :], start=True, stop=True)
                ins.then_inc(lin_ready, 1)

            def exponents(c, g):
                (j, n), k = GROUP[g], g % 2
                if g >= 2 or c >= 1:
                    pe.wait_ge(exps_read[k], GROUPS[k] * c + g // 2)
                for m in range(n):
                    dst = exp_ps[k][:, m * CW:(m + 1) * CW]
                    pe.matmul(dst, order[:, :], adj4[c % 2][:, (j + m) * CW:(j + m + 1) * CW],
                              start=True, stop=False)
                    ins = pe.matmul(dst, later[:, j + m, :], countsT[:, c * CW:(c + 1) * CW],
                                    start=False, stop=True)
                ins.then_inc(exps_made[k], 1)

            for first, w in ((0, w2h), (NQ, w3d)):
                turn_quad(first)
                for i in range(first, first + NQ):
                    if i + 1 < first + NQ:
                        turn_quad(i + 1)
                    linear(i, w)
                if first == 0:
                    pe.wait_ge(lin_read, NQ)
                    pe.wait_ge(counts_copied, NQ)
                    pe.wait_ge(late_made, 4)
                    pe.wait_ge(adj4_loaded[0], 16)
                    for g in range(len(GROUP)):
                        exponents(0, g)
                    for k in range(2):
                        pe.wait_ge(exps_read[k], GROUPS[k])
            pe.wait_ge(lin_read, 2 * NQ)

            def decayed(c, g):
                todo = [(b, j) for b in range(2) for j in range(NB)]
                first, last = (len(todo) * x // len(GROUP) for x in (g, g + 1))
                if g == 0:
                    for k in range(2):
                        pe.wait_ge(exps_read[k], GROUPS[k] * (c + 1))
                    if c >= 2:
                        pe.wait_ge(agg_read, 2 * NC + c - 1)
                for b, j in todo[first:last]:
                    ins = pe.matmul(agg[:, c % 2 * 2 + b, 0:SPL],
                                    w_exp[c % 2][:, j, b * P:(b + 1) * P].bitcast(bf16),
                                    s_spl[:, j, :], start=(j == 0), stop=(j == NB - 1))
                if g == len(GROUP) - 1:
                    ins.then_inc(agg_ready, 1)

            for c in range(1, NC + 1):
                if c < NC:
                    pe.wait_ge(adj4_loaded[c % 2], (c // 2 + 1) * 16)
                for g in range(len(GROUP)):
                    if c < NC:
                        exponents(c, g)
                    decayed(c - 1, g)

        @block.vector
        def _(dve):
            step = Chain(dve, dve_step)
            s = [small[:, k, :] for k in range(16)]

            def root(n):
                dve.wait_ge(root_ready, n + 1)

            dve.memset(hT[D:NW, :], 1.0).then_inc(rows_made, 1)
            dve.memset(hT4[D:NW, :, :], 1.0).then_inc(rows_made, 1)
            dve.memset(w0[D:NW, D:2 * D], 0.0).then_inc(rows_made, 1)
            dve.memset(w1u[0:D, D:2 * D], 0.0).then_inc(rows_made, 1)
            dve.memset(w1u[D:NW, 0:D], 0.0).then_inc(rows_made, 1)
            dve.wait_ge(x_all_loaded, 16)
            sa = [st_all[:, k, :] for k in range(4)]
            step(dve.tensor_reduce(sa[0], x_all[:, :, :], AX, ALU.add))
            step(dve.scalar_tensor_tensor(x_all[:, :, :], wide(sa[0]), -1.0 / D, x_all[:, :, :], ALU.mult, ALU.add))
            step(dve.tensor_tensor(sq_all[:, :, :], x_all[:, :, :], x_all[:, :, :], ALU.mult))
            dve.tensor_reduce(sa[1], sq_all[:, :, :], AX, ALU.add).then_inc(var_ready, 1)
            root(0)
            step(dve.reciprocal(sa[3], sa[2]))

            def norm0(i):
                j, n = QUADS[i]
                if i >= 2:
                    dve.wait_ge(turned, i - 1)
                dve.scalar_tensor_tensor(h_quad[:, i % 2, 0:n], x_all[:, j:j + n], 0.0, wide(sa[3][:, j:j + n]),
                                         ALU.max, ALU.mult).then_inc(h_ready, 1)

            def split(chain, dst, v, rest, last):
                chain(dve.tensor_copy(dst[:, :, 0:D], v))
                chain(dve.tensor_tensor(rest, v, dst[:, :, 0:D], ALU.subtract))
                chain(dve.tensor_copy(dst[:, :, D:2 * D], rest))
                dve.tensor_tensor(dst[:, :, 2 * D:SPL], rest, dst[:, :, D:2 * D], ALU.subtract).then_inc(last, 1)

            norm0(0)
            norm0(1)
            for i, (j, n) in enumerate(QUADS):
                if i + 2 < NQ:
                    norm0(i + 2)
                dve.wait_ge(z_ready, i + 1)
                m = (mm, one)[i % 2][:, 0:n * P].rearrange("p (b n) -> p b n", b=n)
                step.go(dve.tensor_copy(base[:, j:j + n], m[:, :, 0:D]))
                split(step, z_spl[:, j:j + n, 0:SPL], m[:, :, D:2 * D], r_quad[:, 0:n], z_split)

            def layer_norm(v, h, n, event):
                step(dve.tensor_reduce(s[7], v, AX, ALU.add))
                step(dve.scalar_tensor_tensor(t_b[:, :, :], wide(s[7]), -1.0 / D, v, ALU.mult, ALU.add))
                step(dve.tensor_tensor(t_c[:, :, :], t_b[:, :, :], t_b[:, :, :], ALU.mult))
                dve.tensor_reduce(s[8], t_c[:, :, :], AX, ALU.add).then_inc(var_ready, 1)
                root(n)
                step(dve.reciprocal(s[10], s[9]))
                dve.scalar_tensor_tensor(h, t_b[:, :, :], 0.0, wide(s[10]), ALU.max, ALU.mult) \
                    .then_inc(event, 1)

            def sum_parts(v):
                return v.rearrange("p b (k d) -> p b d k", k=3)

            def layer12(c, q):
                step.turn(start1, c, STEPS1)
                dve.wait_ge(agg_ready, c + 1)
                got = agg[:, 2 * q:2 * q + 2, :]
                step.go(dve.tensor_tensor(rows[:, :, :], got[:, :, 0:SPL], pair(z_spl, c)[:, :, 0:SPL], ALU.add))
                step.go(dve.tensor_copy(pair(counts, c), got[:, :, SPL:SPL + NB]))
                dve.tensor_reduce(deg[:, bass.ds(2 * c, 2)], got[:, :, SPL:SPL + NB], AX, ALU.add) \
                    .then_inc(agg_read, 1)
                dve.wait_ge(agg_read, c + 1)
                step.go(dve.tensor_scalar(s[1], deg[:, bass.ds(2 * c, 2)], 1.0, 1.0, ALU.add, ALU.max))
                step(dve.tensor_reduce(t_a[:, :, :], sum_parts(rows[:, :, :]), AX, ALU.add))
                step(dve.reciprocal(s[2], s[1]))
                step(dve.tensor_tensor(t_a[:, :, :], t_a[:, :, :], wide(s[2]), ALU.mult))
                step(dve.tensor_tensor(t_a[:, :, :], t_a[:, :, :], pair(base, c), ALU.add))
                step(dve.scalar_tensor_tensor(t_b[:, :, :], t_a[:, :, :], 0.0, t_a[:, :, :], ALU.max, ALU.mult))
                dve.tensor_reduce(s[3], t_b[:, :, :], AX, ALU.add).then_inc(var_ready, 1)
                root(2 * c + 1)
                step(dve.tensor_scalar(s[5], s[4], L2_EPS, None, ALU.max))
                step(dve.reciprocal(s[6], s[5]))
                step(dve.scalar_tensor_tensor(t_b[:, :, :], t_a[:, :, :], 0.0, wide(s[6]), ALU.max, ALU.mult))
                dve.wait_ge(x_in_sem[c % 3], (c // 3 + 1) * 16)
                step(dve.tensor_tensor(x_in[:, c % 3], t_b[:, :, :], x_in[:, c % 3], ALU.add))
                if not isinstance(c, int) or c >= 1:
                    dve.wait_ge(turned, NQ + c)
                layer_norm(x_in[:, c % 3], t_c[:, :, :], 2 * c + 2, h_ready)
                assert step.n == STEPS1, step.n

            start1 = step.n
            for c in range(NC):
                layer12(c, c % 2)

            def layer2(c, q):
                step.turn(start2, c, STEPS2)
                dve.wait_ge(agg_ready, NC + c + 1)
                dve.tensor_reduce(t_a[:, :, :], sum_parts(agg[:, 2 * q:2 * q + 2, 0:SPL]), AX, ALU.add) \
                    .then_inc(agg_read, 1)
                dve.wait_ge(agg_read, NC + c + 1)
                step(dve.tensor_tensor(t_a[:, :, :], t_a[:, :, :], pair(base, c), ALU.add))
                dve.tensor_scalar(pair(base, c), t_a[:, :, :], 0.0, None, ALU.add).then_inc(x2_ready, 1)
                layer_norm(t_a[:, :, :], pair(h2, c), 2 * NC + 1 + c, h2_ready)
                dve.wait_ge(h2_ready, c + 1)
                step(dve.tensor_tensor(t_b[:, :, :], pair(h2, c), pair(h2, c), ALU.mult))
                step(dve.tensor_reduce(x2[:, 2 * c:2 * c + 2], t_b[:, :, :], AX, ALU.add))
                assert step.n == STEPS2, step.n

            start2 = start1 + STEPS1 * NC
            for c in range(NC):
                layer2(c, 1 - c % 2)

            start3 = start2 + STEPS2 * NC
            step.turn(start3, 0, 0)
            dve.wait_ge(h2_ready, NC)
            step(dve.memset(zero_row[:, :], 0.0))
            step(dve.memset(norms[:, :, 3:6], 1.0))
            n2 = x2[:, :].unsqueeze(2)
            rest, rest3 = pn[:, 0, :], pn[:, 0, :].unsqueeze(2)
            step(dve.tensor_copy(norms[:, :, 0:1], n2))
            step.go(dve.tensor_copy(norms[:, :, 6:7], n2))
            step(dve.tensor_tensor(rest3, n2, norms[:, :, 0:1], ALU.subtract))
            step.go(dve.tensor_copy(norms[:, :, 1:2], rest3))
            step(dve.tensor_copy(norms[:, :, 7:8], rest3))
            step(dve.tensor_tensor(norms[:, :, 2:3], rest3, norms[:, :, 1:2], ALU.subtract))
            dve.tensor_copy(norms[:, :, 8:9], norms[:, :, 2:3]).then_inc(norms_ready, 1)
            step(dve.tensor_scalar(x_b[:, :], x2[:, :], -1.0, 1.0, ALU.mult, ALU.add))
            for c in range(NC):
                dve.wait_ge(parts_turned, c + 1)
                got = side_ps[c % 2]
                for k, far in ((0, far12), (1, far31)):
                    ins = dve.tensor_copy(far[:, c * CW:(c + 1) * CW].rearrange("p (b n) -> p b n", b=2),
                                          got[:, :, k, :])
                    step.go(ins) if k == 0 else ins.then_inc(far_copied, 1)
                if c >= NORMS_AT:
                    j, n = QUADS[c - NORMS_AT]
                    dve.wait_ge(norms_turned, c - NORMS_AT + 1)
                    dve.tensor_copy(own_n[:, j * P:(j + n) * P], one[0:KN, 0:n * P]).then_inc(own_n_copied, 1)
            for k in range(1, NQ, 2):
                j, n = QUADS[k]
                dve.wait_ge(row_ready, k + 1)
                dve.tensor_copy(x_b_row[:, j * P:(j + n) * P], agg[:, k % 4, 0:n * P]).then_inc(row_copied[1], 1)
            dve.wait_ge(far_copied, NC)
            for far in (far12, far31):
                dve.tensor_copy(far[:, NP:EXB * P], far[:, 0:EXB * P - NP]).then_inc(wrapped, 1)
            dve.wait_ge(xrow_ready, 2)
            step.go(dve.tensor_scalar(xrow[:, 0:NB, D:NW], n2, 1.0, None, ALU.add))
            dve.tensor_scalar(xrow[:, NB:EXB, D:NW], x2[:, 0:EXB - NB].unsqueeze(2), 1.0, None, ALU.add) \
                .then_inc(wrapped, 1)
            dve.wait_ge(far_n_copied, NQ)
            dve.tensor_copy(far_n[:, NP:EXB * P], far_n[:, 0:EXB * P - NP]).then_inc(wrapped, 1)
            dve.wait_ge(row_copied[0], (NQ + 1) // 2)
            dve.wait_ge(row_copied[1], NQ // 2)
            dve.tensor_copy(x_b_row[:, NP:EXB * P], x_b_row[:, 0:EXB * P - NP]).then_inc(wrapped, 1)
            dve.wait_ge(wrapped, 5)
            start3 += step.n
            step.turn(start3, 0, 0)

            def front(s, r, u):
                t = 4 * s + 2 * r + u
                if not isinstance(t, int) or t >= 1:
                    dve.wait_ge(prod_ready, t)
                dve.wait_ge(dist_ready, t + 1)
                d, w = den[:, 0:UW[u]], dist_ps[:, 0:UW[u]]
                step(dve.scalar_tensor_tensor(d, x_b_row[:, bass.ds(s * CW + UO[u] * P, UW[u])],
                                              x_b[:, bass.ds(2 * s + r, 1)], w, ALU.mult, ALU.add))
                if not isinstance(t, int) or t >= 2:
                    dve.wait_ge(nrm_ready, t - 1)
                dve.scalar_tensor_tensor(dist[u][:, :], d, NORM_FLOOR, w, ALU.mult, ALU.max) \
                    .then_inc(apart, 1)

            def product(s, r, u):
                t = 4 * s + 2 * r + u
                dve.wait_ge(apart, t + 1)
                if not isinstance(t, int) or t >= 4:
                    dve.wait_ge(tr_ready, 2 * t - 6)
                    dve.wait_ge(dir_ready[u], 2 * s + r - 1)
                dve.scalar_tensor_tensor(gain[2 * r + u][:, :], den[:, 0:UW[u]], MIN_NORM, dist[u][:, :],
                                         ALU.max, ALU.mult).then_inc(prod_ready, 1)

            def back(s, r, u):
                t = 4 * s + 2 * r + u
                dve.wait_ge(atanh_ready, t + 1)
                dve.scalar_tensor_tensor(gain[2 * r + u][:, :], atanh[u][:, :], 0.5, gain[2 * r + u][:, :],
                                         ALU.mult, ALU.mult).then_inc(gain_ready, 1)
                dve.wait_ge(gain_ready, t + 1)
                dve.wait_ge(mask_loaded[u][r], 16 * s + 16)
                if u == 1:
                    if not isinstance(t, int) or t >= 2:
                        dve.wait_ge(dir_used, t - 1)
                    dve.tensor_tensor(p_dir[u][:, :], gain[2 * r + u][:, :], mask[u][r][:, 0:UW[u]], ALU.mult) \
                        .then_inc(dir_ready[u], 1)

            def back_turned(s, r, u):
                t = 4 * s + 2 * r + u
                if not isinstance(t, int) or t >= 2:
                    dve.wait_ge(tr_used, t - 1)
                for h in range(2):
                    dve.wait_ge(turn_ready, 2 * t + h + 1)
                    dve.tensor_tensor(p_tr[u][:, 3 * h * P:3 * (h + 1) * P], turn_ps[:, h, 0:3 * P],
                                      mask[u][r][:, UW[u] + 3 * h * P:UW[u] + 3 * (h + 1) * P], ALU.mult) \
                        .then_inc(tr_ready, 1)

            def units(s):
                for k in range(4):
                    step.turn(start3, 4 * s + k, 1)
                    front(s, k // 2, k % 2)
                    if not isinstance(s, int) or s >= 1:
                        back_turned(s - 1, k // 2, k % 2)
                    product(s, k // 2, k % 2)
                    if k == 3:
                        back(s, 0, 0)
                    elif not isinstance(s, int) or s >= 1:
                        back(s - 1, (k + 1) // 2, (k + 1) % 2)

            start3 += step.n
            units(0)
            units(1)
            with dve.Fori(2, NC) as s:
                units(s)
            start3 += UNITS
            step.turn(start3, 0, 0)
            back_turned(NC - 1, 0, 0)
            for k in range(1, 4):
                back(NC - 1, k // 2, k % 2)
                back_turned(NC - 1, k // 2, k % 2)

            p = [pn[:, k, :] for k in range(8)]
            step(dve.tensor_scalar(p[3], deg[:, :], 1e-8, None, ALU.max))
            step(dve.reciprocal(p[4], p[3]))
            step(dve.tensor_scalar(p[3], x_b[:, :], MIN_NORM, None, ALU.max))
            step(dve.tensor_tensor(p[3], p[3], p[4], ALU.mult))

            dve.wait_ge(tr_used, UNITS)
            u_sum, tmp, lin = post[0], post[1], post[2]
            for b in range(4):
                at, n = 7 * b, min(7, NB - 7 * b)
                got = agg[:, b, 0:504].rearrange("p (k n) -> p k n", k=7)[:, 0:n]
                step.go(dve.tensor_tensor(tmp[:, at:at + n, :], got[:, :, 0:D], h2[:, at:at + n, :], ALU.mult))
                step.go(dve.tensor_tensor(u_sum[:, at:at + n, :], got[:, :, 0:D], wide(x_b[:, at:at + n]), ALU.mult))
                ins = dve.tensor_copy(pn[:, 0, at:at + n].unsqueeze(2), got[:, :, D:NW])
                step(ins) if b < 3 else ins.then_inc(sums_read, 1)
            dve.wait_ge(sums_read, 1)
            step(dve.tensor_reduce(p[1], tmp[:, :, :], AX, ALU.add))
            step(dve.scalar_tensor_tensor(p[2], p[1], -2.0, p[0], ALU.mult, ALU.add))
            def rows_out(i, v, scale, op0):
                j, n = QUADS[i % NQ]
                if i >= 2:
                    dve.wait_ge(quad_turned, i - 1)
                dve.scalar_tensor_tensor(row_quad[:, i % 2, 0:n], v[:, j:j + n], 0.0 if op0 == ALU.max else 1.0,
                                         wide(scale[:, j:j + n]), op0, ALU.mult).then_inc(quad_ready, 1)

            def product(i):
                dve.wait_ge(lin_ready, i + 1)
                n = QUADS[i % NQ][1]
                return (mm, one)[i % 2][:, 0:n * D].rearrange("p (b n) -> p b n", b=n)

            def take(i):
                j, n = QUADS[i]
                dve.tensor_tensor(lin[:, j:j + n], product(i), b2_all[:, :].unsqueeze(1).broadcast_to([P, n, D]),
                                  ALU.add).then_inc(lin_read, 1)
                dve.wait_ge(lin_read, i + 1)
                step(dve.tensor_tensor(tmp[:, j:j + n], lin[:, j:j + n], lin[:, j:j + n], ALU.mult))
                ins = dve.tensor_reduce(p[5][:, j:j + n], tmp[:, j:j + n], AX, ALU.add)
                step.go(ins) if i < NQ - 1 else ins.then_inc(var_ready, 1)

            def ahead(first, out_of, into):
                out_of(first)
                out_of(first + 1)
                for i in range(first, first + NQ):
                    if i + 2 < first + NQ:
                        out_of(i + 2)
                    into(i)

            dve.wait_ge(late_loaded, 64)
            def agg_out(i):
                j, n = QUADS[i]
                step(dve.tensor_tensor(t_quad[:, 0:n], h2[:, j:j + n], wide(p[2][:, j:j + n]), ALU.mult))
                step(dve.tensor_tensor(u_sum[:, j:j + n], u_sum[:, j:j + n], t_quad[:, 0:n], ALU.subtract))
                rows_out(i, u_sum, p[3], ALU.mult)

            ahead(0, agg_out, take)
            root(3 * NC + 1)
            dve.tensor_scalar(p[6], p[6], MIN_NORM, None, ALU.max).then_inc(nv_ready, 1)
            dve.wait_ge(nv_ready, 1)
            step(dve.reciprocal(p[5], p[6]))
            dve.wait_ge(tanh3_ready, 1)
            step(dve.tensor_tensor(p[7], p[7], p[5], ALU.mult))
            step(dve.tensor_tensor(lin[:, :, :], lin[:, :, :], wide(p[7]), ALU.mult))
            dve.tensor_tensor(base[:, :, :], base[:, :, :], lin[:, :, :], ALU.add).then_inc(x3_ready, 1)
            dve.wait_ge(x3_ready, 1)

            hc, sq4 = post[0], post[1]
            step(dve.tensor_reduce(p[0], base[:, :, :], AX, ALU.add))
            step(dve.scalar_tensor_tensor(hc[:, :, :], wide(p[0]), -1.0 / D, base[:, :, :], ALU.mult, ALU.add))
            step(dve.tensor_tensor(sq4[:, :, :], hc[:, :, :], hc[:, :, :], ALU.mult))
            dve.tensor_reduce(p[3], sq4[:, :, :], AX, ALU.add).then_inc(var_ready, 1)
            root(3 * NC + 2)
            step(dve.reciprocal(p[3], p[2]))

            def split4(i):
                j, n = QUADS[i % NQ]
                split(step, s_spl[:, j:j + n], product(i), t_quad[:, 0:n], lin_read)

            ahead(NQ, lambda i: rows_out(i, hc, p[3], ALU.max), split4)
            start4 = start3 + step.n

            def layer4(c, q):
                for g, (j, n) in enumerate(GROUP):
                    if g % 2 == 1:
                        dve.wait_ge(exps_made[1], GROUPS[1] * c + g // 2 + 1)
                        if g == 1 and (not isinstance(c, int) or c >= 2):
                            dve.wait_ge(agg_ready, 2 * NC + c - 1)
                        dve.tensor_scalar(w_exp[q][:, j:j + n, :].rearrange("p j n -> p (j n)"),
                                          exp_ps[1][:, 0:n * CW], W_SHIFT, 0.0, ALU.add, ALU.max) \
                            .then_inc(exps_read[1], 1)

            def result(c, q):
                step.turn(start4, c, 1)
                dve.wait_ge(agg_ready, 2 * NC + c + 1)
                dve.tensor_reduce(t_a[:, :, :], sum_parts(agg[:, 2 * q:2 * q + 2, 0:SPL]), AX, ALU.add) \
                    .then_inc(agg_read, 1)
                dve.wait_ge(agg_read, 2 * NC + c + 1)
                if not isinstance(c, int) or c >= 2:
                    dve.wait_ge(out_sent[q], c // 2 * 16)
                step(dve.tensor_scalar(t_a[:, :, :], t_a[:, :, :], 2.0 ** (127 - HORIZON), None, ALU.mult))
                dve.tensor_tensor(o_buf[:, q], t_a[:, :, :], pair(base, c), ALU.add).then_inc(out_made, 1)
                dve.wait_ge(out_made, c + 1)

            def both(c, q):
                layer4(c, q)
                if not isinstance(c, int) or c >= 2:
                    result(c - 2, q)

            dve.wait_ge(lin_read, 2 * NQ)
            dve.wait_ge(bias_added, 1)
            both(1, 1)
            both(2, 0)
            both(3, 1)
            with dve.Fori(4, NC - 1, 2) as c:
                both(c, 0)
                both(c + 1, 1)
            both(NC - 1, 0)
            result(NC - 2, 1)
            result(NC - 1, 0)


def kernel(x, adj, L0_gnn_W, L0_gnn_b, L1_gnn_t, L1_gnn_B, L1_gnn_W1, L1_gnn_b1, L1_gnn_W2, L1_gnn_b2,
           L2_gnn_weight, L2_gnn_bias, L3_gnn_weight, L3_gnn_bias):
    import numpy as np
    import concourse.bacc as bacc
    from concourse.bass_utils import run_bass_kernel_spmd

    x, adj = np.asarray(x), np.asarray(adj)
    rows = np.zeros((NP, D), x.dtype)
    rows[:N] = x
    rows = rows.reshape(NB, P, D).transpose(1, 0, 2)
    turned = np.zeros((NP, NP), adj.dtype)
    turned[:N, :N] = adj.T
    cols = turned.reshape(NB, P, NC, CW).transpose(2, 1, 0, 3).reshape(NC, P, NB * CW)
    tiles = turned.reshape(NB, P, NB, P)
    mask = np.empty((NB, P, NB, P), adj.dtype)
    for i in range(NB):
        first = i // 2 * 2
        at = 0
        for u in range(2):
            for k in range(UO[u], UO[u] + UB[u]):
                mask[i, :, at] = tiles[i, :, (first + k) % NB]
                at += 1
            for k in range(UT[u], UT[u] + 6):
                mask[i, :, at] = tiles[(first + k) % NB, :, i]
                at += 1
    w0, w1 = np.asarray(L0_gnn_W), np.asarray(L1_gnn_W1)
    laid = dict(x=rows, adj_cols=cols, adj_mask=mask.reshape(NB, P, NP),
                w_self=w0[:D], w_neigh=w0[D:], b0=np.asarray(L0_gnn_b).reshape(1, D),
                t1=np.stack([np.asarray(L1_gnn_t), np.ones_like(L1_gnn_t)]), bt1=np.asarray(L1_gnn_B).T, w11=w1,
                b11=np.asarray(L1_gnn_b1).reshape(1, HID), w12=np.asarray(L1_gnn_W2),
                b12=np.asarray(L1_gnn_b2).reshape(1, D),
                w_hyp=np.asarray(L2_gnn_weight), b_hyp=np.asarray(L2_gnn_bias).reshape(1, D),
                w_dec=np.asarray(L3_gnn_weight), b_dec=np.asarray(L3_gnn_bias).reshape(1, D))
    nc = bacc.Bacc("TRN2", target_bir_lowering=False, num_devices=1)
    arrays, args = {}, []
    for name, a in laid.items():
        arrays[f"in_{name}"] = np.ascontiguousarray(a)
        args.append(nc.dram_tensor(f"in_{name}", a.shape, mybir.dt.from_np(a.dtype), kind="ExternalInput").ap())
    args.append(nc.dram_tensor("out_rows", (P, NB, D), mybir.dt.float32, kind="ExternalOutput").ap())
    gnn_stack(nc, *args)
    got = run_bass_kernel_spmd(nc, [arrays], core_ids=[0]).results[0]["out_rows"]
    return np.ascontiguousarray(np.asarray(got).transpose(1, 0, 2).reshape(NP, D)[:N])
```
